# Optimizing a Trainium2 kernel written in Bass

```python
import numpy as np
import jax
import jax.numpy as jnp

def _softmax(x, axis=-1):
    return jax.nn.softmax(x, axis=axis)

def _gelu(x):
    return jax.nn.gelu(x, approximate=True)

def _silu(x):
    return jax.nn.silu(x)

def _sigmoid(x):
    return jax.nn.sigmoid(x)

def _layernorm(x, axis=-1, eps=1e-05):
    m = jnp.mean(x, axis=axis, keepdims=True)
    v = jnp.var(x, axis=axis, keepdims=True)
    return (x - m) / jnp.sqrt(v + eps)

def _scatter_add(tgt, idx, src, axis=0):
    return tgt.at[idx].add(src)

def _segment_sum(src, seg, n):
    return jax.ops.segment_sum(src, seg, n)
kernel_name = 'mk_gnn_resnorm_d2_gnn_r8_c1e341'

def setup_inputs(seed: int=0):
    np.random.seed(seed)
    _w = jnp.asarray

    def _rec_inputs():
        import jax
        import jax.numpy as jnp
        _gk = jax.random.key(seed)
        x = -0.0003713 + 1 * jax.random.normal(jax.random.fold_in(_gk, 1), (6250, 256), jnp.float32)
        _s = jax.random.randint(jax.random.fold_in(_gk, 2), (50000,), 0, 6250, jnp.int32)
        _d = jax.random.randint(jax.random.fold_in(_gk, 3), (50000,), 0, 6250, jnp.int32)
        _loop = jnp.arange(6250, dtype=jnp.int32)
        src = jnp.concatenate([_s, _d, _loop])
        dst = jnp.concatenate([_d, _s, _loop])
        _o = jnp.argsort(dst, stable=True)
        src = src[_o]
        dst = dst[_o]
        edge_type_16 = jax.random.randint(jax.random.fold_in(_gk, 13), (106250,), 0, 16, jnp.int32)
        return (x, src, dst, edge_type_16)
    x, src, dst, edge_type_16 = _rec_inputs()

    def _L0_gnn_setup():
        import jax, jax.numpy as jnp
        import numpy as np
        N_NODES = 6250
        N_EDGES = 100000
        HDIM = 256
        NUMRELS = 16

        def _gru_cell(x, h, w_ih, w_hh, b_ih, b_hh):
            gi = x @ w_ih.T + b_ih
            gh = h @ w_hh.T + b_hh
            i_r, i_z, i_n = jnp.split(gi, 3, axis=-1)
            h_r, h_z, h_n = jnp.split(gh, 3, axis=-1)
            r = jax.nn.sigmoid(i_r + h_r)
            z = jax.nn.sigmoid(i_z + h_z)
            n = jnp.tanh(i_n + r * h_n)
            return (1.0 - z) * n + z * h
        key = jax.random.key(seed)
        ks = jax.random.split(key, 9)
        h = jax.random.normal(ks[0], (N_NODES, HDIM), dtype=jnp.float32)
        relvectors = jax.random.normal(ks[1], (NUMRELS, HDIM), dtype=jnp.float32)
        s = 1.0 / np.sqrt(HDIM)
        w_ih = jax.random.uniform(ks[2], (3 * HDIM, HDIM), minval=-s, maxval=s, dtype=jnp.float32)
        w_hh = jax.random.uniform(ks[3], (3 * HDIM, HDIM), minval=-s, maxval=s, dtype=jnp.float32)
        b_ih = jax.random.uniform(ks[4], (3 * HDIM,), minval=-s, maxval=s, dtype=jnp.float32)
        b_hh = jax.random.uniform(ks[5], (3 * HDIM,), minval=-s, maxval=s, dtype=jnp.float32)
        edge_src = jax.random.randint(ks[6], (N_EDGES,), 0, N_NODES, dtype=jnp.int32)
        edge_dst = jax.random.randint(ks[7], (N_EDGES,), 0, N_NODES, dtype=jnp.int32)
        edge_rel = jax.random.randint(ks[8], (N_EDGES,), 0, NUMRELS, dtype=jnp.int32)
        return {'h': h, 'relvectors': relvectors, 'w_ih': w_ih, 'w_hh': w_hh, 'b_ih': b_ih, 'b_hh': b_hh, 'edge_src': edge_src, 'edge_dst': edge_dst, 'edge_rel': edge_rel}
    _L0_gnn_all = _L0_gnn_setup()
    _L0_gnn_in = {k: v for k, v in _L0_gnn_all.items() if k in ('relvectors', 'w_ih', 'w_hh', 'b_ih', 'b_hh')}
    del _L0_gnn_all

    def _L1_gnn_setup():
        import jax, jax.numpy as jnp
        import numpy as np
        key = jax.random.key(seed)
        k1, k2, k3 = jax.random.split(key, 3)
        N, E, D_IN, D_OUT = (12500, 400000, 256, 256)
        x = jax.random.normal(k1, (N, D_IN), dtype=jnp.float32)
        W = jax.random.normal(k2, (D_OUT, D_IN), dtype=jnp.float32) * (1.0 / np.sqrt(D_IN))
        edge_index = jax.random.randint(k3, (2, E), 0, N, dtype=jnp.int32)
        return {'x': x, 'W': W, 'edge_index': edge_index}
    _L1_gnn_all = _L1_gnn_setup()
    _L1_gnn_in = {k: v for k, v in _L1_gnn_all.items() if k in ('W',)}
    del _L1_gnn_all
    return {'x': x, 'src': src, 'dst': dst, 'edge_type_16': edge_type_16, 'L0_gnn_relvectors': _L0_gnn_in['relvectors'], 'L0_gnn_w_ih': _L0_gnn_in['w_ih'], 'L0_gnn_w_hh': _L0_gnn_in['w_hh'], 'L0_gnn_b_ih': _L0_gnn_in['b_ih'], 'L0_gnn_b_hh': _L0_gnn_in['b_hh'], 'L1_gnn_W': _L1_gnn_in['W']}

def reference(x, src, dst, edge_type_16, L0_gnn_relvectors, L0_gnn_w_ih, L0_gnn_w_hh, L0_gnn_b_ih, L0_gnn_b_hh, L1_gnn_W):
    import jax
    import jax.numpy as jnp

    def _L0_gnn_ref(h, relvectors, w_ih, w_hh, b_ih, b_hh, edge_src, edge_dst, edge_rel):
        import jax, jax.numpy as jnp
        import numpy as np
        N_NODES = 6250
        N_EDGES = 100000
        HDIM = 256
        NUMRELS = 16

        def _gru_cell(x, h, w_ih, w_hh, b_ih, b_hh):
            gi = x @ w_ih.T + b_ih
            gh = h @ w_hh.T + b_hh
            i_r, i_z, i_n = jnp.split(gi, 3, axis=-1)
            h_r, h_z, h_n = jnp.split(gh, 3, axis=-1)
            r = jax.nn.sigmoid(i_r + h_r)
            z = jax.nn.sigmoid(i_z + h_z)
            n = jnp.tanh(i_n + r * h_n)
            return (1.0 - z) * n + z * h
        msg = h[edge_src] + relvectors[edge_rel]
        red = jax.ops.segment_sum(msg, edge_dst, num_segments=h.shape[0])
        return _gru_cell(red, h, w_ih, w_hh, b_ih, b_hh)

    def _L1_gnn_ref(x, W, edge_index):
        import jax, jax.numpy as jnp
        import numpy as np
        N = x.shape[0]
        loops = jnp.arange(N, dtype=edge_index.dtype)
        src = jnp.concatenate([edge_index[0], loops])
        dst = jnp.concatenate([edge_index[1], loops])
        deg = jax.ops.segment_sum(jnp.ones_like(src, dtype=x.dtype), src, num_segments=N)
        deg_rsqrt = jax.lax.rsqrt(deg)
        vals = deg_rsqrt[src] * deg_rsqrt[dst]
        h = x @ W.T
        msgs = vals[:, None] * h[dst]
        out = jax.ops.segment_sum(msgs, src, num_segments=N)
        return out
    edge_index = jnp.stack([src, dst])
    x = _layernorm(x + _L0_gnn_ref(x, L0_gnn_relvectors, L0_gnn_w_ih, L0_gnn_w_hh, L0_gnn_b_ih, L0_gnn_b_hh, src, dst, edge_type_16), axis=-1)
    x = _layernorm(x + _L1_gnn_ref(x, L1_gnn_W, edge_index), axis=-1)
    return x

_drawn_inputs = setup_inputs


def setup_inputs(seed=0):
    import zlib

    import numpy as np

    out = dict(_drawn_inputs(seed))
    spreads = {}
    factors = {'L0_gnn_b_ih': 8.0, 'L0_gnn_b_hh': 8.0}
    for name, (base, spread) in spreads.items():
        noise = np.random.default_rng([zlib.crc32(name.encode()), seed]).standard_normal(out[name].shape)
        drawn = base * np.exp(spread * noise) if base else spread * noise
        out[name] = jnp.asarray(drawn.astype(out[name].dtype))
    for name, factor in factors.items():
        out[name] = (out[name] * factor).astype(out[name].dtype)
    return out
```

```python
from contextlib import ExitStack

import concourse.bass as bass
from concourse import mybir

F32, BF16, I32 = mybir.dt.float32, mybir.dt.bfloat16, mybir.dt.int32
ALU, ACT = mybir.AluOpType, mybir.ActivationFunctionType
AX_X = mybir.AxisListType.X

N, D, E, R = 6250, 256, 106250, 16
P = 128
NT = -(-N // P)
LAST = N - (NT - 1) * P
B = NT + 1
C = 832
PAD_KEY = NT * P
REAL_P = E // C
REAL_C = E - REAL_P * C
J = 880
JP = J + 16
KC = -(-C // P)
KROWS = [min(P, C - k * P) for k in range(KC)]
H = 8
HALVES = J // H
G3 = 3 * D
MAGIC = 1.5 * 2.0 ** 23
EPS = 1e-5
assert -(-E // P) + NT - 1 <= J and J % (2 * H) == 0 and C * P >= E and C % 16 == 0


class Count:

    def __init__(self, sem):
        self.sem, self.base, self.k = sem, 0, 0

    def value(self):
        return self.base + self.k

    def add(self, ins):
        ins.then_inc(self.sem, 1)
        self.k += 1

    def enter(self, i, per):
        self.first, self.per = self.value(), per
        self.base, self.k = i * per + self.first, 0

    def leave(self, trips):
        assert self.k == self.per, self.k
        self.base, self.k = self.first + trips * self.per, 0


def build(nc, x, src, dst, etype, rel, w_ih, w_hh, b_ih, b_hh, w1, out, table0, table1, gdram):
    ctx = ExitStack()
    with ctx:
        def sb(name, shape, dt=F32):
            return ctx.enter_context(nc.sbuf_tensor(name, shape, dt))

        def sem(name):
            return ctx.enter_context(nc.semaphore(name))

        ps = ctx.enter_context(nc.psum_tensor("ps", [P, 8, 512], F32))

        iota = sb("iota", [P, JP])
        iota_p = sb("iota_p", [P, KC])
        iota_bf = sb("iota_bf", [P, P], BF16)
        ident = sb("ident", [P, P])
        ones = sb("ones", [P, P])
        neg_half = sb("neg_half", [P, NT])
        zero_bf = sb("zero_bf", [P, P], BF16)
        sums1 = sb("sums1", [P, B * D])
        taken = [0]

        def early(*shape, dt=F32):
            size = 1
            for d in shape:
                size *= d
            words = size * (2 if dt == BF16 else 4) // 4
            part = sums1[:, taken[0]:taken[0] + words]
            taken[0] += words
            assert taken[0] <= NT * D
            part = part if dt == F32 else part.bitcast(dt)
            if len(shape) == 2:
                part = part.rearrange("p (a b) -> p a b", a=shape[0])
            if len(shape) == 3:
                part = part.rearrange("p (a b c) -> p a b c", a=shape[0], b=shape[1])
            return part

        src_i = early(C, dt=I32)
        dst_i = early(C, dt=I32)
        next_i = early(C, dt=I32)
        typ_i = early(C, dt=I32)
        pos_i = typ_i
        hi = early(C)
        lo = early(C)
        mask = early(C)
        scan = early(C)
        pos = early(C)
        pay = early(C, 2)
        stage_i = early(2, H, dt=I32)
        stage_v = early(2, H, 2)
        oh_lo = early(2, H, P, dt=BF16)
        oh_hi = early(2, H, NT, dt=BF16)
        brow = early(2 * G3)[0:1]
        before = early(P)
        counts = sb("counts", [P, B])
        base = sb("base", [P, B])
        flag = sb("flag", [P, 1])
        flag_i = sb("flag_i", [P, 1], I32)
        deg_rs = sb("deg_rs", [P, NT])
        row = sb("row", [P, 8, B])
        col = sb("col", [P, 2])
        colrep = sb("colrep", [P, P])
        node_t = sb("node_t", [P, JP])
        key_lo = sb("key_lo", [P, JP])
        gidx = sb("gidx", [P, JP])
        gtyp = sb("gtyp", [P, JP])
        offs = sb("offs", [1, JP], I32)
        ids = sb("ids", [P, 2, H], I32)
        rows = sb("rows", [P, 2 * H, D])
        onehot = sb("onehot", [P, 2 * H, P])
        onetyp = sb("onetyp", [P, 2 * H, P])
        chunk = rows[:, :, :].rearrange("p a b -> p (a b)")[:, 0:KC * P * 2].rearrange(
            "p (k s w) -> p k s w", k=KC, w=2)
        sel = onehot[:, :, :].rearrange("p a b -> p (a b)")[:, 0:2 * J].rearrange("p (a b) -> p a b", a=2)
        spare = onetyp[:, :, :].rearrange("p a b -> p (a b)")
        past, edge_t = spare[:, 0:J], spare[:, J:2 * J]
        sums0 = sb("sums0", [P, B * 3 * P])
        wT = sb("wT", [P, 2, 2, G3])
        w1T = sb("w1T", [P, 2, D])
        rel_s = sb("rel_s", [R, D])
        wnat = sums0[:, 0:2 * G3 // P * D].rearrange("p (a k d) -> p a k d", a=2, d=D)
        w1nat = sums0[:, 2 * G3 // P * D:(2 * G3 // P + 2) * D].rearrange("p (k d) -> p k d", d=D)
        bias = sb("bias", [P, 4 * D])
        xt = sb("xt", [P, 2, D])
        gt = sb("gt", [P, 2, D])
        ot = gt
        xT, redT, tA, tB, hn, y = (spare[:, m * D:m * D + D] for m in range(6))
        gate = spare[:, 6 * D:8 * D]
        x1c = sb("x1c", [P, D])
        x1T = sb("x1T", [P, D])
        st = sb("st", [P, 6])
        mv = sb("mv", [P, 2])
        ve = sb("ve", [P, 1])
        rs = sb("rs", [P, 1])

        def per_layer(name):
            return [sem(f"{name}{n}") for n in range(2)]

        s_const, s_zero, s_pad, s_edges = sem("s_const"), sem("s_zero"), sem("s_pad"), sem("s_edges")
        s_w, s_brow = sem("s_w"), sem("s_brow")
        s_v = sem("s_v")
        s_sort = sem("s_sort")
        s_ones = sem("s_ones")
        s_wtr, s_wcp, s_bias_mm, s_bias = sem("s_wtr"), sem("s_wcp"), sem("s_bias_mm"), sem("s_bias")
        s_flag_in, s_flag_mm, s_flag, s_nat = sem("s_flag_in"), sem("s_flag_mm"), sem("s_flag"), sem("s_nat")
        s_cnt, s_cnt_mm, s_pos, s_stage = map(per_layer, ("s_cnt", "s_cnt_mm", "s_pos", "s_stage"))
        s_slot = [[sem(f"s_slot{n}_{k}") for k in range(2 * H)] for n in range(2)]
        s_table = per_layer("s_table")
        s_deg_oh, s_deg_mm, s_deg1, s_degr = sem("s_deg_oh"), sem("s_deg_mm"), sem("s_deg1"), sem("s_degr")
        s_chunk, s_past, s_plan_mm, s_plan_rd = sem("s_chunk"), sem("s_past"), sem("s_plan_mm"), sem("s_plan_rd")
        s_sel, s_exp = sem("s_sel"), sem("s_exp")
        s_rows = [sem(f"s_rows{k}") for k in range(2 * H)]
        s_ids, s_oh, s_mm, s_acc = map(per_layer, ("s_ids", "s_oh", "s_mm", "s_acc"))
        s_go = sem("s_go")
        s_vgo = sem("s_vgo")
        s_x, s_gst, s_ost = per_layer("s_xt"), per_layer("s_gst"), per_layer("s_ost")
        s_xtr, s_xT, s_rel, s_red, s_gates = (sem(n) for n in ("s_xtr", "s_xT", "s_rel", "s_red", "s_gates"))
        s_rz, s_rzs, s_npre, s_n = (sem(n) for n in ("s_rz", "s_rzs", "s_npre", "s_n"))
        s_ve, s_rs = sem("s_ve"), sem("s_rs")
        s_x1, s_x1tr, s_x1T, s_h, s_g, s_o = (sem(n) for n in ("s_x1", "s_x1tr", "s_x1T", "s_h", "s_g", "s_o"))

        tables = (table0, table1)
        pay_v = pay[:, :, :].rearrange("p c w -> p (c w)")
        JB = J // 2

        def weight_tiles():
            for a in range(2):
                for k in range(G3 // P):
                    for c in range(2):
                        yield wT[:, a, c, k * P:(k + 1) * P]
            for k in range(2):
                for c in range(2):
                    yield w1T[:, c, k * P:(k + 1) * P]

        block = ctx.enter_context(nc.Block())

        @block.sync
        def _(sp):
            for k in range(2):
                sp.sem_inc(s_gst[k], 16)
                sp.sem_inc(s_ost[k], 16)
            for a, w in enumerate((w_ih, w_hh)):
                sp.dma_start(wnat[:, a], w.rearrange("(k p) d -> p k d", p=P)).then_inc(s_w, 16)
            sp.dma_start(w1nat, w1.rearrange("(k p) d -> p k d", p=P)).then_inc(s_w, 16)
            sp.dma_start(rel_s[:, :], rel).then_inc(s_w, 16)
            for a, b in enumerate((b_ih, b_hh)):
                sp.dma_start(brow[0:1, a * G3:(a + 1) * G3], b.rearrange("(a n) -> a n", a=1)).then_inc(s_brow, 16)
            sp.wait_ge(s_pad, 4)
            for t, a, first in ((dst_i, dst, 0), (next_i, dst, 1), (src_i, src, 0), (typ_i, etype, 0)):
                sp.dma_start(t[0:REAL_P, :],
                             a[first:REAL_P * C + first].rearrange("(p c) -> p c", c=C)).then_inc(s_edges, 16)
                sp.dma_start(t[REAL_P:REAL_P + 1, 0:REAL_C - first],
                             a[REAL_P * C + first:E].rearrange("(p c) -> p c", p=1)).then_inc(s_edges, 16)
            for n in range(2):
                sp.wait_ge(s_table[n], 1)
                if n:
                    sp.wait_ge(s_acc[0], J + H)
                for k in range(KC):
                    r = KROWS[k]
                    sp.dma_start(chunk[0:r, k].rearrange("t s w -> t (s w)"),
                                 tables[n][k * P * P:(k * P + r) * P, :].rearrange(
                                     "(t s) w -> t (s w)", s=P)).then_inc(s_chunk, 16)

            def load_x(t, k, rws):
                sp.dma_start(xt[0:rws, k, :], x[bass.ds(t * P, rws), :]).then_inc(s_x[k], 16)

            def store(dest, tile, ready, value, done, t, k, rws):
                sp.wait_ge(ready, value)
                sp.dma_start(dest[bass.ds(t * P, rws), :], tile[0:rws, k, :]).then_inc(done[k], 16)

            load_x(0, 0, P)
            load_x(1, 1, P)
            with sp.Fori(0, NT // 2 - 1) as i:
                for k in range(2):
                    t = i * 2 + k
                    sp.wait_ge(s_x1, t + 1)
                    load_x(t + 2, k, P)
                    store(gdram, gt, s_g, t + 2, s_gst, t, k, P)
            sp.wait_ge(s_x1, NT - 2)
            load_x(NT - 1, 0, LAST)
            for t in range(NT - 3, NT):
                store(gdram, gt, s_g, t + 2, s_gst, t, t % 2, P if t < NT - 1 else LAST)
            with sp.Fori(0, NT // 2) as i:
                for k in range(2):
                    store(out, ot, s_o, i * 2 + (k + 1), s_ost, i * 2 + k, k, P)
            store(out, ot, s_o, NT, s_ost, NT - 1, 0, LAST)
            for k in range(2):
                sp.wait_ge(s_gst[k], (NT + 1 - k) // 2 * 16 + 16)
                sp.wait_ge(s_ost[k], (NT + 1 - k) // 2 * 16 + 16)

        @block.gpsimd
        def _(pool):
            G = nc.gpsimd
            G.memset(src_i[:, :], PAD_KEY).then_inc(s_pad, 1)
            G.memset(dst_i[:, :], PAD_KEY).then_inc(s_pad, 1)
            G.memset(next_i[:, :], PAD_KEY).then_inc(s_pad, 1)
            G.memset(typ_i[:, :], 0).then_inc(s_pad, 1)
            G.memset(ones[:, :], 1.0).then_inc(s_ones, 1)
            G.memset(ident[:, :], 0.0).then_inc(s_ones, 1)
            G.memset(neg_half[:, :], -0.5).then_inc(s_const, 1)
            G.iota(iota[:, :], pattern=[[1, JP]], base=0, channel_multiplier=0,
                   allow_small_or_imprecise_dtypes=True).then_inc(s_const, 1)
            G.iota(iota_p[:, :], pattern=[[P, KC]], base=0, channel_multiplier=1,
                   allow_small_or_imprecise_dtypes=True).then_inc(s_const, 1)
            G.iota(iota_bf[:, :], pattern=[[1, P]], base=0, channel_multiplier=0,
                   allow_small_or_imprecise_dtypes=True).then_inc(s_const, 1)
            pool.wait_ge(s_ones, 2)
            G.affine_select(out=ident[:, :], in_=ident[:, :], compare_op=ALU.not_equal, fill=1.0,
                            base=0, pattern=[[-1, P]], channel_multiplier=1).then_inc(s_const, 1)
            G.affine_select(out=before[:, :], in_=ones[:, :], compare_op=ALU.is_ge, fill=0.0,
                            base=-1, pattern=[[1, P]], channel_multiplier=-1).then_inc(s_const, 1)

            def scatter(n):
                def issue(i):
                    for h in range(2):
                        at = i * (2 * H) + h * H
                        if not (isinstance(i, int) and i == 0):
                            for k in range(h * H, h * H + H):
                                pool.wait_ge(s_slot[n][k], i * 16)
                            pool.sem_inc(s_go, 1)
                        G.tensor_copy(stage_i[:, h, :], pos_i[:, bass.ds(at, H)]).then_inc(s_stage[n], 1)
                        G.tensor_copy(stage_v[:, h].rearrange("p k w -> p (k w)"),
                                      pay_v[:, bass.ds(at * 2, 2 * H)]).then_inc(s_stage[n], 1)
                        pool.wait_ge(s_stage[n], i * 4 + (2 * h + 2))
                        pool.sem_inc(s_go, 1)
                        for k in range(H):
                            pool.indirect_dma_start(
                                tables[n][:, :], bass.IndirectOffsetOnAxis(ap=stage_i[:, h, k:k + 1], axis=0),
                                stage_v[:, h, k, :], None).then_inc(s_slot[n][h * H + k], 16)

                issue(0)
                with pool.Fori(1, C // (2 * H)) as i:
                    issue(i)
                for k in range(2 * H):
                    pool.wait_ge(s_slot[n][k], C // (2 * H) * 16)

            pool.wait_ge(s_flag, 1)
            unsorted = pool.value_load(flag_i[0:1, 0:1], min_val=0, max_val=1)
            pool.wait_ge(s_pos[0], 1)
            with pool.If(unsorted > 0):
                scatter(0)
            with pool.Else():
                pool.dma_start(table0.rearrange("(p c) w -> p (c w)", c=C), pay_v).then_inc(s_nat, 16)
                pool.wait_ge(s_nat, 16)
            pool.sem_inc(s_table[0], 1)
            pool.wait_ge(s_pos[1], 1)
            scatter(1)
            pool.sem_inc(s_table[1], 1)
            pool.wait_ge(s_deg1, 1)
            G.tensor_tensor(deg_rs[:, :], deg_rs[:, :], neg_half[:, :], ALU.pow).then_inc(s_degr, 1)

            def gather(n, source):
                with pool.Fori(0, HALVES // 2) as i:
                    for h in range(2):
                        pool.wait_ge(s_ids[n], i * 2 + (h + 1))
                        pool.sem_inc(s_go, 1)
                        for k in range(H):
                            pool.indirect_dma_start(
                                rows[:, h * H + k, :], None, source,
                                bass.IndirectOffsetOnAxis(ap=ids[:, h, k:k + 1], axis=0)
                            ).then_inc(s_rows[h * H + k], 16)

            def inverse_roots(n):
                with pool.Fori(0, NT) as t:
                    pool.wait_ge(s_ve, t + (n * NT + 1))
                    G.tensor_tensor(rs[:, :], ve[:, :], neg_half[:, 0:1], ALU.pow).then_inc(s_rs, 1)

            gather(0, x[:, :])
            inverse_roots(0)
            for k in range(2):
                pool.wait_ge(s_gst[k], (NT + 1 - k) // 2 * 16 + 16)
            gather(1, gdram[:, :])
            inverse_roots(1)

        @block.vector
        def _(dve):
            V = nc.vector
            own, sort = Count(s_v), Count(s_sort)
            order = [own]

            def note(ins):
                order[0].add(ins)

            def settle():
                dve.wait_ge(order[0].sem, order[0].value())

            def step(ins):
                note(ins)
                settle()

            def rounded(out_ap, in_ap, shift, scale):
                step(V.tensor_scalar(out_ap, in_ap, shift, scale, ALU.add, ALU.mult))
                step(V.tensor_scalar(out_ap, out_ap, MAGIC, None, ALU.add))
                step(V.tensor_scalar(out_ap, out_ap, MAGIC, None, ALU.subtract))

            def floor128(out_ap, in_ap):
                rounded(out_ap, in_ap, -63.5, 1.0 / P)

            def prepare(n):
                key, val = ((dst_i, src_i), (src_i, dst_i))[n]
                step(V.tensor_copy(lo[:, :], key[:, :]))
                note(V.tensor_copy(pay[:, :, 1], lo[:, :]))
                step(V.tensor_copy(scan[:, :], val[:, :]))
                step(V.tensor_scalar(mask[:, :], scan[:, :], float(PAD_KEY), None, ALU.is_lt))
                step(V.tensor_tensor(scan[:, :], scan[:, :], mask[:, :], ALU.mult))
                if n == 0:
                    step(V.tensor_copy(mask[:, :], typ_i[:, :]))
                    step(V.scalar_tensor_tensor(pay[:, :, 0], scan[:, :], float(R), mask[:, :], ALU.mult, ALU.add))
                else:
                    step(V.tensor_scalar(pay[:, :, 0], scan[:, :], float(R), None, ALU.mult))
                floor128(hi[:, :], lo[:, :])
                step(V.scalar_tensor_tensor(lo[:, :], hi[:, :], -float(P), lo[:, :], ALU.mult, ALU.add))
                for b in range(B):
                    note(V.tensor_scalar(mask[:, :], hi[:, :], float(b), None, ALU.is_equal, ALU.add,
                                         accum_out=counts[:, b:b + 1]))
                    settle()
                dve.sem_inc(s_cnt[n], 1)

            def bucket_ends(n):
                dve.wait_ge(s_cnt_mm[n], 1)
                step(V.tensor_copy(row[:, 6, :], ps[:, 0, 0:B]))
                step(V.memset(row[:, 5, :], 0.0))
                step(V.tensor_tensor_scan(row[:, 0, :], row[:, 6, :], row[:, 5, :], 0.0, ALU.add, ALU.add))

            def positions():
                step(V.tensor_tensor(base[:, :], row[:, 0, :], row[:, 6, :], ALU.subtract))
                step(V.tensor_tensor(base[:, :], base[:, :], ps[:, 1, 0:B], ALU.add))
                step(V.memset(pos[:, :], -1.0))
                with dve.Fori(0, B) as b:
                    order[0].enter(b, 4)
                    step(V.tensor_scalar(mask[:, :], hi[:, :], iota[:, bass.ds(b, 1)], None, ALU.is_equal))
                    step(V.tensor_tensor_scan(scan[:, :], mask[:, :], mask[:, :], base[:, bass.ds(b, 1)],
                                              ALU.add, ALU.max))
                    step(V.tensor_tensor(scan[:, :], scan[:, :], mask[:, :], ALU.mult))
                    step(V.tensor_tensor(pos[:, :], pos[:, :], scan[:, :], ALU.add))
                order[0].leave(B)
                step(V.tensor_copy(pos_i[:, :], pos[:, :]))

            def plan(n, width):
                step(V.tensor_tensor(row[:, 1, :], row[:, 0, :], row[:, 6, :], ALU.subtract))
                floor128(row[:, 2, :], row[:, 1, :])
                step(V.tensor_scalar(row[:, 1, :], row[:, 0, :], 1.0, None, ALU.subtract))
                floor128(row[:, 3, :], row[:, 1, :])
                step(V.tensor_tensor(row[:, 3, :], row[:, 3, :], row[:, 2, :], ALU.subtract))
                step(V.tensor_scalar(row[:, 3, :], row[:, 3, :], 1.0, 1.0, ALU.add, ALU.max))
                step(V.tensor_tensor_scan(row[:, 4, :], row[:, 3, :], row[:, 5, :], 0.0, ALU.add, ALU.add))
                step(V.tensor_tensor(row[:, 3, :], row[:, 3, :], row[:, 4, :], ALU.subtract))
                step(V.tensor_tensor(row[:, 3, :], row[:, 3, :], row[:, 2, :], ALU.add))
                step(V.memset(row[:, 2, :], 0.0))
                step(V.tensor_tensor(row[:, 2, 0:NT - 1], row[:, 3, 1:NT], row[:, 3, 0:NT - 1], ALU.subtract))
                for c, r in ((0, 4), (1, 2)):
                    step(V.tensor_tensor(row[0:NT, 7, 0:NT], row[0:NT, r, 0:NT], ident[0:NT, 0:NT], ALU.mult))
                    step(V.reduce_sum(col[0:NT, c:c + 1], row[0:NT, 7, 0:NT], axis=AX_X))
                note(V.tensor_scalar(past[0:NT, :], iota[0:NT, 0:J], col[0:NT, 0:1], None, ALU.is_ge))
                step(V.tensor_scalar(colrep[0:NT, :], ones[0:NT, :], col[0:NT, 1:2], None, ALU.mult))
                dve.sem_inc(s_past, 1)
                dve.wait_ge(s_plan_mm, n + 1)
                note(V.memset(node_t[:, J:JP], float(NT)))
                for c in range(2):
                    part = slice(c * JB, c * JB + JB)
                    note(V.tensor_copy(node_t[:, part], ps[:, c, 0:JB]))
                    note(V.tensor_tensor(edge_t[:, part], ps[:, 2 + c, 0:JB], iota[:, part], ALU.add))
                settle()
                step(V.tensor_scalar(offs[0:1, :], node_t[0:1, :], float(width), None, ALU.mult))
                for k in range(KC):
                    if n or k >= 2:
                        dve.wait_ge(s_exp, n * KC + k - 1)
                    V.tensor_scalar(sel[:, k % 2, :], edge_t[:, :], iota_p[:, k:k + 1], None,
                                    ALU.is_equal).then_inc(s_sel, 1)
                dve.wait_ge(s_exp, (n + 1) * KC)
                note(V.memset(gidx[:, J:JP], 0.0))
                note(V.memset(gtyp[:, J:JP], 0.0))
                note(V.memset(key_lo[:, J:JP], -1.0))
                for c in range(2):
                    part = slice(c * JB, c * JB + JB)
                    note(V.tensor_copy(gtyp[:, part], ps[:, 4 + c, 0:JB]))
                    note(V.scalar_tensor_tensor(key_lo[:, part], node_t[:, part], -float(P), ps[:, 6 + c, 0:JB],
                                                ALU.mult, ALU.add))
                settle()
                rounded(gidx[:, 0:J], gtyp[:, 0:J], -7.5, 1.0 / R)
                step(V.scalar_tensor_tensor(gtyp[:, 0:J], gidx[:, 0:J], -float(R), gtyp[:, 0:J], ALU.mult, ALU.add))

            def walk(n, sums, width):
                for _ in range(H):
                    dve.sem_inc(s_acc[n], 1)

                def stage(s, h):
                    V.tensor_scalar(ids[:, h, :], gidx[:, bass.ds(s * H, H)], 0.0, None, ALU.add).then_inc(s_ids[n], 1)

                def hots(s, h):
                    for k in range(H):
                        V.tensor_scalar(onehot[:, h * H + k, :], iota[:, 0:P], key_lo[:, bass.ds(s * H + k, 1)],
                                        None, ALU.is_equal).then_inc(s_oh[n], 1)
                        if n == 0:
                            V.tensor_scalar(onetyp[:, h * H + k, :], iota[:, 0:P], gtyp[:, bass.ds(s * H + k, 1)],
                                            None, ALU.is_equal).then_inc(s_oh[n], 1)

                stage(0, 0)
                stage(1, 1)
                hots(0, 0)
                with dve.Fori(0, HALVES // 2) as i:
                    for h in range(2):
                        s = i * 2 + h
                        at = [dve.value_load(offs[0:1, bass.ds(s * H + k, 1)], min_val=0, max_val=NT * width)
                              for k in range(H)]
                        hots(s + 1, 1 - h)
                        for k in range(H):
                            dve.wait_ge(s_mm[n], s * H + (k + 1))
                            dve.wait_ge(s_acc[n], s * H + (k + H))
                            dest = sums[:, bass.ds(at[k], width)]
                            V.tensor_tensor(dest, dest, ps[:, k, 0:width], ALU.add).then_inc(s_acc[n], 1)
                        stage(s + 2, h)
                dve.wait_ge(s_acc[n], J + H)

            def moments(value):
                step(V.bn_stats(st[:, :], y[:, :]))
                dve.sem_inc(s_vgo, 1)
                step(V.bn_aggr(mv[:, :], st[:, :]))
                V.tensor_scalar(ve[:, :], mv[:, 1:2], EPS, None, ALU.add).then_inc(s_ve, 1)
                dve.wait_ge(s_rs, value)

            def gru(t, k):
                dve.wait_ge(s_rel, t + 1)
                dve.wait_ge(s_gates, t + 1)
                V.tensor_tensor(redT[:, :], sums0[:, bass.ds(t * (3 * P), D)], ps[:, 1, 0:D],
                                ALU.add).then_inc(s_red, 1)
                dve.wait_ge(s_gates, t + 2)
                V.tensor_tensor(gate[:, :], ps[:, 2, :], bias[:, 0:2 * D], ALU.add).then_inc(s_rz, 1)
                note(V.tensor_tensor(tA[:, :], ps[:, 3, 0:D], bias[:, 2 * D:3 * D], ALU.add))
                note(V.tensor_tensor(hn[:, :], ps[:, 3, D:2 * D], bias[:, 3 * D:4 * D], ALU.add))
                settle()
                dve.wait_ge(s_rzs, t + 1)
                step(V.scalar_tensor_tensor(tB[:, :], gate[:, 0:D], 1.0, hn[:, :], ALU.add, ALU.mult))
                V.scalar_tensor_tensor(tA[:, :], tB[:, :], 0.5, tA[:, :], ALU.mult, ALU.add).then_inc(s_npre, 1)
                dve.wait_ge(s_n, t + 1)
                step(V.tensor_tensor(y[:, :], xt[:, k, :], tB[:, :], ALU.subtract))
                step(V.scalar_tensor_tensor(y[:, :], gate[:, D:2 * D], 1.0, y[:, :], ALU.add, ALU.mult))
                step(V.scalar_tensor_tensor(y[:, :], y[:, :], 0.5, tB[:, :], ALU.mult, ALU.add))
                step(V.tensor_tensor(y[:, :], y[:, :], xt[:, k, :], ALU.add))
                moments(t + 1)
                note(V.tensor_scalar(sums0[:, bass.ds(t * (3 * P), D)], y[:, :], mv[:, 0:1], rs[:, :],
                                     ALU.subtract, ALU.mult))
                dve.wait_ge(s_x1tr, t + 1)
                V.tensor_scalar(x1c[:, :], y[:, :], mv[:, 0:1], rs[:, :], ALU.subtract, ALU.mult).then_inc(s_x1, 1)
            GRU_STEPS = 10

            def put_g(t, stored, k):
                dve.wait_ge(s_h, t + 2)
                note(V.tensor_scalar(sums1[:, bass.ds(t * D, D)], ps[:, 5, 0:D], deg_rs[:, bass.ds(t, 1)], None,
                                     ALU.mult))
                dve.wait_ge(s_gst[k], stored * 16 + 16)
                V.tensor_scalar(gt[:, k, :], ps[:, 5, 0:D], deg_rs[:, bass.ds(t, 1)], None,
                                ALU.mult).then_inc(s_g, 1)

            def finish(t, stored, k):
                step(V.scalar_tensor_tensor(y[:, :], sums1[:, bass.ds(t * D, D)], deg_rs[:, bass.ds(t, 1)],
                                            sums0[:, bass.ds(t * (3 * P), D)], ALU.mult, ALU.add))
                moments(t + (NT + 1))
                dve.wait_ge(s_ost[k], stored * 16 + 16)
                V.tensor_scalar(ot[:, k, :], y[:, :], mv[:, 0:1], rs[:, :], ALU.subtract, ALU.mult).then_inc(s_o, 1)
                dve.wait_ge(s_o, t + 1)
            FINISH_STEPS = 3

            V.memset(zero_bf[:, :], 0.0).then_inc(s_zero, 1)
            dve.sem_inc(s_red, 1)
            dve.sem_inc(s_npre, 1)
            dve.sem_inc(s_g, 1)
            dve.wait_ge(s_const, 6)
            dve.wait_ge(s_edges, 128)
            note(V.tensor_copy(lo[:, :], dst_i[:, :]))
            step(V.tensor_copy(hi[:, :], next_i[:, :]))
            step(V.tensor_tensor(mask[:, :], lo[:, :], hi[:, :], ALU.is_gt))
            step(V.reduce_sum(flag[:, 0:1], mask[:, :], axis=AX_X))
            dve.sem_inc(s_flag_in, 1)
            prepare(0)
            dve.wait_ge(s_flag_mm, 1)
            step(V.tensor_scalar(flag_i[0:1, :], ps[0:1, 2, 0:1], 0.0, None, ALU.is_gt))
            dve.sem_inc(s_flag, 1)
            bucket_ends(0)
            unsorted = dve.value_load(flag_i[0:1, 0:1], min_val=0, max_val=1)
            with dve.If(unsorted > 0):
                order[0] = sort
                positions()
                order[0] = own
            dve.sem_inc(s_pos[0], 1)
            plan(0, 3 * P)
            prepare(1)
            bucket_ends(1)
            positions()
            dve.sem_inc(s_pos[1], 1)
            dve.sem_inc(s_deg_mm, 2 * H)
            with dve.Fori(0, C // (2 * H)) as i:
                for k in range(2 * H):
                    at = i * (2 * H) + k
                    dve.wait_ge(s_deg_mm, at + 1)
                    V.tensor_scalar(oh_lo[:, k // H, k % H, :], iota_bf[:, :], lo[:, bass.ds(at, 1)], None,
                                    ALU.is_equal).then_inc(s_deg_oh, 1)
                    V.tensor_scalar(oh_hi[:, k // H, k % H, :], iota_bf[:, 0:NT], hi[:, bass.ds(at, 1)], None,
                                    ALU.is_equal).then_inc(s_deg_oh, 1)
            dve.wait_ge(s_deg_mm, C + 2 * H + 1)
            V.tensor_scalar(deg_rs[:, :], ps[:, 7, 0:NT], 1.0, None, ALU.add).then_inc(s_deg1, 1)
            dve.wait_ge(s_degr, 1)
            dve.wait_ge(s_wtr, 28)
            note(V.memset(sums0[:, :], 0.0))
            step(V.memset(sums1[:, NT * D:B * D], 0.0))
            walk(0, sums0, 3 * P)
            dve.wait_ge(s_bias, 3)
            gru(0, 0)
            with dve.Fori(0, NT // 2) as i:
                own.enter(i, 2 * (GRU_STEPS + 1))
                for k in range(2):
                    gru(i * 2 + (k + 1), 1 - k)
                    put_g(i * 2 + k, i, k)
            own.leave(NT // 2)
            put_g(NT - 1, NT // 2, 0)
            settle()
            plan(1, D)
            walk(1, sums1, D)
            with dve.Fori(0, NT // 2) as i:
                own.enter(i, 2 * FINISH_STEPS)
                for k in range(2):
                    finish(i * 2 + k, i, k)
            own.leave(NT // 2)
            finish(NT - 1, NT // 2, 0)

        @block.scalar
        def _(act):
            A = nc.scalar
            act.sem_inc(s_xT, 1)
            act.sem_inc(s_x1T, 1)
            act.sem_inc(s_wcp, 4)
            at = 0
            for dest in weight_tiles():
                act.wait_ge(s_wtr, at + 1)
                A.copy(dest, ps[:, 4 + at % 4, 0:P]).then_inc(s_wcp, 1)
                at += 1
            for m, (bank, first, size) in enumerate(((4, 0, 2 * D), (5, 2 * D, D), (6, 3 * D, D))):
                act.wait_ge(s_bias_mm, m + 1)
                A.copy(bias[:, first:first + size], ps[:, bank, 0:size]).then_inc(s_bias, 1)

            def front(t):
                act.wait_ge(s_xtr, t + 1)
                act.wait_ge(s_gates, t + 1)
                A.copy(xT[:, :], ps[:, 0, 0:D]).then_inc(s_xT, 1)
                act.wait_ge(s_rz, t + 1)
                A.activation(gate[:, :], gate[:, :], ACT.Tanh, scale=0.5).then_inc(s_rzs, 1)
                act.wait_ge(s_npre, t + 2)
                A.activation(tB[:, :], tA[:, :], ACT.Tanh).then_inc(s_n, 1)

            def back(t):
                act.wait_ge(s_x1tr, t + 2)
                act.wait_ge(s_h, t + 1)
                A.copy(x1T[:, :], ps[:, 4, 0:D]).then_inc(s_x1T, 1)

            front(0)
            with act.Fori(0, NT // 2) as i:
                for k in range(2):
                    front(i * 2 + (k + 1))
                    back(i * 2 + k)
            back(NT - 1)

        @block.tensor
        def _(pe):
            M = nc.tensor
            pe.sem_inc(s_gates, 1)
            pe.sem_inc(s_x1tr, 1)
            pe.sem_inc(s_h, 1)
            pe.wait_ge(s_const, 6)
            pe.wait_ge(s_w, 64)
            blocks = [wnat[:, a, k, c * P:(c + 1) * P] for a in range(2) for k in range(G3 // P) for c in range(2)]
            blocks += [w1nat[:, k, c * P:(c + 1) * P] for k in range(2) for c in range(2)]
            for at, b in enumerate(blocks):
                pe.wait_ge(s_wcp, at + 1)
                M.transpose(ps[:, 4 + at % 4, 0:P], b, ident[:, :]).then_inc(s_wtr, 1)
            pe.wait_ge(s_wcp, len(blocks) + 4)
            pe.wait_ge(s_brow, 32)
            one = ones[0:1, :]
            M.matmul(ps[:, 4, :], one, brow[0:1, 0:2 * D], start=True, stop=False)
            M.matmul(ps[:, 4, :], one, brow[0:1, G3:G3 + 2 * D], start=False, stop=True).then_inc(s_bias_mm, 1)
            M.matmul(ps[:, 5, 0:D], one, brow[0:1, 2 * D:G3], start=True, stop=True).then_inc(s_bias_mm, 1)
            M.matmul(ps[:, 6, 0:D], one, brow[0:1, G3 + 2 * D:2 * G3], start=True, stop=True).then_inc(s_bias_mm, 1)
            pe.wait_ge(s_flag_in, 1)
            M.matmul(ps[:, 2, 0:1], ones[:, :], flag[:, 0:1], start=True, stop=True).then_inc(s_flag_mm, 1)

            def count(n):
                pe.wait_ge(s_cnt[n], 1)
                M.matmul(ps[:, 0, 0:B], ones[:, :], counts[:, :], start=True, stop=True)
                M.matmul(ps[:, 1, 0:B], before[:, :], counts[:, :], start=True, stop=True).then_inc(s_cnt_mm[n], 1)

            def plan(n):
                pe.wait_ge(s_past, n + 1)
                for q, lhs in enumerate((ones, colrep)):
                    for c in range(2):
                        last = M.matmul(ps[:, 2 * q + c, 0:JB], lhs[0:NT, :], past[0:NT, c * JB:c * JB + JB],
                                        start=True, stop=True)
                last.then_inc(s_plan_mm, 1)
                pe.wait_ge(s_chunk, 16 * KC * (n + 1))
                pe.wait_ge(s_bias, 3)
                for k in range(KC):
                    pe.wait_ge(s_sel, n * KC + k + 1)
                    r = KROWS[k]
                    for w in range(2):
                        for c in range(2):
                            last = M.matmul(ps[:, 4 + 2 * w + c, 0:JB], chunk[0:r, k, :, w],
                                            sel[0:r, k % 2, c * JB:c * JB + JB], start=(k == 0), stop=(k == KC - 1))
                    last.then_inc(s_exp, 1)

            def walk(n):
                hots = 2 if n == 0 else 1
                with pe.Fori(0, HALVES // 2) as i:
                    for h in range(2):
                        for k in range(H):
                            q, slot = i * (2 * H) + h * H + k, h * H + k
                            pe.wait_ge(s_acc[n], q + 1)
                            pe.wait_ge(s_oh[n], (q + 1) * hots)
                            pe.wait_ge(s_rows[slot], i * 16 + (n * HALVES // 2 * 16 + 16))
                            if n == 0:
                                for c in range(2):
                                    M.matmul(ps[:, k, c * P:c * P + P], rows[:, slot, c * P:c * P + P],
                                             onehot[:, slot, :], start=True, stop=True)
                                last = M.matmul(ps[:, k, D:D + P], onetyp[:, slot, :], onehot[:, slot, :],
                                                start=True, stop=True)
                            else:
                                last = M.matmul(ps[:, k, 0:D], onehot[:, slot, :], rows[:, slot, :],
                                                start=True, stop=True)
                            last.then_inc(s_mm[n], 1)

            def front(t, loaded, k):
                pe.wait_ge(s_x[k], loaded * 16 + 16)
                pe.wait_ge(s_xT, t + 1)
                for c in range(2):
                    last = M.transpose(ps[:, 0, c * P:c * P + P], xt[:, k, c * P:c * P + P], ident[:, :])
                last.then_inc(s_xtr, 1)
                pe.wait_ge(s_red, t + 1)
                for c in range(2):
                    last = M.matmul(ps[:, 1, c * P:c * P + P], rel_s[:, c * P:c * P + P],
                                    sums0[0:R, bass.ds(t * (3 * P) + D, P)], start=True, stop=True)
                last.then_inc(s_rel, 1)
                pe.wait_ge(s_npre, t + 1)
                pe.wait_ge(s_xT, t + 2)
                pe.wait_ge(s_red, t + 2)
                parts = [(m[:, c * P:c * P + P], wT[:, a, c, :]) for a, m in ((1, xT), (0, redT)) for c in range(2)]
                for q, (lhs, w) in enumerate(parts):
                    M.matmul(ps[:, 2, :], lhs, w[:, 0:2 * D], start=(q == 0), stop=(q == 3))
                for a, cols in ((1, slice(D, 2 * D)), (0, slice(0, D))):
                    for c in range(2):
                        lhs, w = parts[(1 - a) * 2 + c]
                        last = M.matmul(ps[:, 3, cols], lhs, w[:, 2 * D:G3], start=(c == 0), stop=(c == 1))
                last.then_inc(s_gates, 1)

            def back(t):
                pe.wait_ge(s_x1, t + 1)
                pe.wait_ge(s_x1T, t + 1)
                for c in range(2):
                    last = M.transpose(ps[:, 4, c * P:c * P + P], x1c[:, c * P:c * P + P], ident[:, :])
                last.then_inc(s_x1tr, 1)
                pe.wait_ge(s_g, t + 1)
                pe.wait_ge(s_x1T, t + 2)
                for c in range(2):
                    last = M.matmul(ps[:, 5, 0:D], x1T[:, c * P:c * P + P], w1T[:, c, :], start=(c == 0), stop=(c == 1))
                last.then_inc(s_h, 1)

            count(0)
            plan(0)
            count(1)
            pe.wait_ge(s_zero, 1)
            M.matmul(ps[:, 7, 0:NT], zero_bf[:, :], zero_bf[:, 0:NT], start=True, stop=False)
            with pe.Fori(0, C // (2 * H)) as i:
                for k in range(2 * H):
                    pe.wait_ge(s_deg_oh, i * (4 * H) + (2 * k + 2))
                    M.matmul(ps[:, 7, 0:NT], oh_lo[:, k // H, k % H, :], oh_hi[:, k // H, k % H, :],
                             start=False, stop=False).then_inc(s_deg_mm, 1)
            M.matmul(ps[:, 7, 0:NT], zero_bf[:, :], zero_bf[:, 0:NT], start=False, stop=True).then_inc(s_deg_mm, 1)
            pe.wait_ge(s_degr, 1)
            walk(0)
            front(0, 0, 0)
            with pe.Fori(0, NT // 2) as i:
                for k in range(2):
                    front(i * 2 + (k + 1), i + k, 1 - k)
                    back(i * 2 + k)
            back(NT - 1)
            plan(1)
            walk(1)


_INS = ['x', 'src', 'dst', 'edge_type_16', 'L0_gnn_relvectors', 'L0_gnn_w_ih', 'L0_gnn_w_hh', 'L0_gnn_b_ih',
        'L0_gnn_b_hh', 'L1_gnn_W']


def kernel(**inputs):
    import numpy as _np
    import concourse.bacc as _bacc
    from concourse import mybir as _mybir
    from concourse.bass_utils import run_bass_kernel_spmd as _run

    nc = _bacc.Bacc("TRN2", target_bir_lowering=False, num_devices=1)
    arrays, args = {}, []
    for name in _INS:
        a = _np.ascontiguousarray(inputs[name])
        arrays[f"in_{name}_dram"] = a
        args.append(nc.dram_tensor(f"in_{name}_dram", a.shape, _mybir.dt.from_np(a.dtype), kind="ExternalInput").ap())
    f32 = _mybir.dt.float32
    args.append(nc.dram_tensor("out_0_dram", (N, D), f32, kind="ExternalOutput").ap())
    for name, shape in (("table0", (C * P, 2)), ("table1", (C * P, 2)), ("gdram", (N, D))):
        args.append(nc.dram_tensor(name, shape, f32, kind="Internal").ap())
    build(nc, *args)
    r = _run(nc, [arrays], core_ids=[0])
    return r.results[0]["out_0_dram"]
```

```python
from contextlib import ExitStack

import concourse.bass as bass
from concourse import mybir

F32, BF16, I32 = mybir.dt.float32, mybir.dt.bfloat16, mybir.dt.int32
ALU, ACT = mybir.AluOpType, mybir.ActivationFunctionType
AX_X = mybir.AxisListType.X

N, D, E, R = 6250, 256, 106250, 16
P = 128
NT = -(-N // P)
LAST = N - (NT - 1) * P
B = NT + 1
C = 832
PAD_KEY = NT * P
REAL_P = E // C
REAL_C = E - REAL_P * C
H = 8
NG = C // H
J = NG + NT - 1
S = 4
KC = -(-C // P)
KROWS = [min(P, C - k * P) for k in range(KC)]
W0 = D + R
RANKS = NG // 2
G3 = 3 * D
MAGIC = 1.5 * 2.0 ** 23
EPS = 1e-5
assert J % 2 == 0 and C * P >= E and C % (S * H) == 0 and B <= RANKS


class Count:

    def __init__(self, sem):
        self.sem, self.base, self.k = sem, 0, 0

    def value(self):
        return self.base + self.k

    def add(self, ins):
        ins.then_inc(self.sem, 1)
        self.k += 1

    def enter(self, i, per):
        self.first, self.per = self.value(), per
        self.base, self.k = i * per + self.first, 0

    def leave(self, trips):
        assert self.k == self.per, self.k
        self.base, self.k = self.first + trips * self.per, 0


def build(nc, x, src, dst, etype, rel, w_ih, w_hh, b_ih, b_hh, w1, out, table0, table1, gdram):
    ctx = ExitStack()
    with ctx:
        def sb(name, shape, dt=F32):
            return ctx.enter_context(nc.sbuf_tensor(name, shape, dt))

        def sem(name):
            return ctx.enter_context(nc.semaphore(name))

        ps = ctx.enter_context(nc.psum_tensor("ps", [P, 8, 512], F32))

        iota = sb("iota", [P, J])
        iota_p = sb("iota_p", [P, 1])
        iota_bf = sb("iota_bf", [P, P], BF16)
        ident = sb("ident", [P, P])
        ones = sb("ones", [P, P])
        neg_half = sb("neg_half", [P, NT])
        zero_bf = sb("zero_bf", [P, P], BF16)
        sums1 = sb("sums1", [P, B * D])
        taken = [0]

        def early(*shape, dt=F32):
            size = 1
            for d in shape:
                size *= d
            words = size * (2 if dt == BF16 else 4) // 4
            part = sums1[:, taken[0]:taken[0] + words]
            taken[0] += words
            assert taken[0] <= NT * D
            part = part if dt == F32 else part.bitcast(dt)
            if len(shape) == 2:
                part = part.rearrange("p (a b) -> p a b", a=shape[0])
            if len(shape) == 3:
                part = part.rearrange("p (a b c) -> p a b c", a=shape[0], b=shape[1])
            return part

        src_i = early(C, dt=I32)
        dst_i = early(C, dt=I32)
        typ_i = early(C, dt=I32)
        hi1 = early(C)
        lo1 = early(C)
        mask = early(C)
        scan = early(C)
        pos = early(C)
        pay1 = sb("pay1", [P, C, 2])[:, :, :]
        pos1_i = sb("pos1_i", [P, C], I32)[:, :]
        pos_is = (typ_i, pos1_i)
        stage_i = sb("stage_i", [P, 2, H], I32)
        stage_v = sb("stage_v", [P, 2, H, 2])
        oh_lo = early(2, H, P, dt=BF16)
        oh_hi = early(2, H, NT, dt=BF16)
        before = early(P)
        counts = sb("counts", [P, 2, B])
        flag = sb("flag", [P, 1])
        flag_i = sb("flag_i", [P, 1], I32)
        deg_rs = sb("deg_rs", [P, NT])
        rows = sb("rows", [P, S * H * D])
        chunk = rows[:, 0:KC * P * 2].rearrange("p (k s w) -> p k s w", k=KC, w=2)
        at0 = KC * P * 2
        pay0 = rows[:, at0:at0 + 2 * C].rearrange("p (c w) -> p c w", w=2)
        hi0 = rows[:, at0 + 2 * C:at0 + 3 * C]
        next_i = rows[:, at0 + 3 * C:at0 + 4 * C].bitcast(I32)
        brow = rows[0:1, at0 + 4 * C:at0 + 4 * C + 2 * G3]
        his, pays = (hi0, hi1), (pay0, pay1)
        rowset = sb("rowset", [P, 2, 8, B])
        base = sb("base", [P, RANKS])
        col = sb("col", [P, 2])
        colrep = sb("colrep", [P, P])
        past = sb("past", [P, J])
        node_t = sb("node_t", [P, J])
        node_p = sb("node_p", [P, J + 2])
        grp_t = sb("grp_t", [P, J])
        grp_m = sb("grp_m", [P, J])
        upto = sb("upto", [P, 1])
        steps_i = sb("steps_i", [1, J + 2, 4], I32)
        steps_v = steps_i[:, :, :].rearrange("p j w -> p (j w)")
        tbuf = rows[:, at0:at0 + C]
        free_i = sb("free_i", [1, P], I32)
        tkey = sb("tkey", [P, C])
        tidx = sb("tidx", [P, C], I32)
        ttyp = sb("ttyp", [P, C])
        ids = sb("ids", [P, S, H], I32)
        klo = sb("klo", [P, 2, H])
        onehot = sb("onehot", [P, 2, H, P])
        onetyp = sb("onetyp", [P, 2, H, R])
        sums0 = sb("sums0", [P, B * W0])
        wT = sb("wT", [P, 2, 2, G3])
        w1T = sb("w1T", [P, 2, D])
        rel_s = sb("rel_s", [R, D])
        wnat = sums0[:, 0:2 * G3 // P * D].rearrange("p (a k d) -> p a k d", a=2, d=D)
        w1nat = sums0[:, 2 * G3 // P * D:(2 * G3 // P + 2) * D].rearrange("p (k d) -> p k d", d=D)
        bias = sb("bias", [P, 4 * D])
        xt = sb("xt", [P, 2, D])
        gt = sb("gt", [P, 2, D])
        ot = gt
        xT, redT, tA, tB, hn, y = (rows[:, m * D:m * D + D] for m in range(16, 22))
        gate = rows[:, 22 * D:24 * D]
        red = rows[:, 24 * D:24 * D + W0]
        cnT = rows[0:R, 26 * D:26 * D + P]
        x1c = sb("x1c", [P, D])
        x1T = sb("x1T", [P, D])
        st = sb("st", [P, 6])
        mv = sb("mv", [P, 2])
        ve = sb("ve", [P, 1])
        rs = sb("rs", [P, 1])

        def per_layer(name):
            return [sem(f"{name}{n}") for n in range(2)]

        s_const, s_zero, s_pad, s_edges = sem("s_const"), sem("s_zero"), sem("s_pad"), sem("s_edges")
        s_w, s_brow = sem("s_w"), sem("s_brow")
        s_v = sem("s_v")
        s_sort = sem("s_sort")
        s_ones = sem("s_ones")
        s_wtr, s_wcp, s_bias_mm, s_bias = sem("s_wtr"), sem("s_wcp"), sem("s_bias_mm"), sem("s_bias")
        s_flag_in, s_flag_mm, s_flag, s_nat = sem("s_flag_in"), sem("s_flag_mm"), sem("s_flag"), sem("s_nat")
        s_cnt, s_cnt_mm, s_pos, s_stage = map(per_layer, ("s_cnt", "s_cnt_mm", "s_pos", "s_stage"))
        s_hi1, s_prod = sem("s_hi1"), sem("s_prod")
        s_slot = [[sem(f"s_slot{n}_{k}") for k in range(2 * H)] for n in range(2)]
        s_table = per_layer("s_table")
        s_deg_oh, s_deg_mm, s_deg1, s_degr = sem("s_deg_oh"), sem("s_deg_mm"), sem("s_deg1"), sem("s_degr")
        s_grp, s_free, s_klo = map(per_layer, ("s_grp", "s_free", "s_klo"))
        s_upto, s_upto_mm, s_rkrel, s_cnT = sem("s_upto"), sem("s_upto_mm"), sem("s_rkrel"), sem("s_cnT")
        s_redr, s_redt = sem("s_redr"), sem("s_redt")
        s_chunk, s_past, s_plan_mm, s_plan_rd = sem("s_chunk"), sem("s_past"), sem("s_plan_mm"), sem("s_plan_rd")
        s_exp = sem("s_exp")
        s_rows = [sem(f"s_rows{k}") for k in range(S * H)]
        s_ids, s_oh, s_mm, s_acc = map(per_layer, ("s_ids", "s_oh", "s_mm", "s_acc"))
        s_go = sem("s_go")
        s_vgo = sem("s_vgo")
        s_x, s_gst, s_ost = per_layer("s_xt"), per_layer("s_gst"), per_layer("s_ost")
        s_xtr, s_xT, s_rel, s_red, s_gates = (sem(n) for n in ("s_xtr", "s_xT", "s_rel", "s_red", "s_gates"))
        s_rz, s_rzs, s_npre, s_n = (sem(n) for n in ("s_rz", "s_rzs", "s_npre", "s_n"))
        s_ve, s_rs = sem("s_ve"), sem("s_rs")
        s_x1, s_x1tr, s_x1T, s_h, s_g, s_o = (sem(n) for n in ("s_x1", "s_x1tr", "s_x1T", "s_h", "s_g", "s_o"))

        tables = (table0, table1)
        def weight_tiles():
            for a in range(2):
                for k in range(G3 // P):
                    for c in range(2):
                        yield wT[:, a, c, k * P:(k + 1) * P]
            for k in range(2):
                for c in range(2):
                    yield w1T[:, c, k * P:(k + 1) * P]

        block = ctx.enter_context(nc.Block())

        @block.sync
        def _(sp):
            for k in range(2):
                sp.sem_inc(s_gst[k], 16)
                sp.sem_inc(s_ost[k], 16)
            for a, w in enumerate((w_ih, w_hh)):
                sp.dma_start(wnat[:, a], w.rearrange("(k p) d -> p k d", p=P)).then_inc(s_w, 16)
            sp.dma_start(w1nat, w1.rearrange("(k p) d -> p k d", p=P)).then_inc(s_w, 16)
            sp.dma_start(rel_s[:, :], rel).then_inc(s_w, 16)
            for a, b in enumerate((b_ih, b_hh)):
                sp.dma_start(brow[0:1, a * G3:(a + 1) * G3], b.rearrange("(a n) -> a n", a=1)).then_inc(s_brow, 16)
            sp.wait_ge(s_pad, 4)
            for t, a, first in ((dst_i, dst, 0), (next_i, dst, 1), (src_i, src, 0), (typ_i, etype, 0)):
                sp.dma_start(t[0:REAL_P, :],
                             a[first:REAL_P * C + first].rearrange("(p c) -> p c", c=C)).then_inc(s_edges, 16)
                sp.dma_start(t[REAL_P:REAL_P + 1, 0:REAL_C - first],
                             a[REAL_P * C + first:E].rearrange("(p c) -> p c", p=1)).then_inc(s_edges, 16)
            def load_table(n):
                sp.wait_ge(s_table[n], 1)
                for k in range(KC):
                    r = KROWS[k]
                    sp.dma_start(chunk[0:r, k].rearrange("t s w -> t (s w)"),
                                 tables[n][k * P * P:(k * P + r) * P, :].rearrange(
                                     "(t s) w -> t (s w)", s=P)).then_inc(s_chunk, 16)

            def free_groups(n):
                sp.wait_ge(s_plan_rd, n + 1)
                with sp.Fori(0, NG) as g:
                    pairs = sp.value_load(free_i[0:1, bass.ds(g, 1)], min_val=1, max_val=J)
                    sp.wait_ge(s_mm[n], pairs)
                    sp.sem_inc(s_free[n], 1)

            def load_x(t, k, rws):
                sp.dma_start(xt[0:rws, k, :], x[bass.ds(t * P, rws), :]).then_inc(s_x[k], 16)

            def store(dest, tile, ready, value, done, t, k, rws):
                sp.wait_ge(ready, value)
                sp.dma_start(dest[bass.ds(t * P, rws), :], tile[0:rws, k, :]).then_inc(done[k], 16)

            load_x(0, 0, P)
            load_x(1, 1, P)
            load_table(0)
            free_groups(0)
            with sp.Fori(0, NT // 2 - 1) as i:
                for k in range(2):
                    t = i * 2 + k
                    sp.wait_ge(s_x1, t + 1)
                    load_x(t + 2, k, P)
                    store(gdram, gt, s_g, t + 2, s_gst, t, k, P)
            sp.wait_ge(s_x1, NT - 2)
            load_x(NT - 1, 0, LAST)
            for t in range(NT - 3, NT):
                store(gdram, gt, s_g, t + 2, s_gst, t, t % 2, P if t < NT - 1 else LAST)
            load_table(1)
            free_groups(1)
            with sp.Fori(0, NT // 2) as i:
                for k in range(2):
                    store(out, ot, s_o, i * 2 + (k + 1), s_ost, i * 2 + k, k, P)
            store(out, ot, s_o, NT, s_ost, NT - 1, 0, LAST)
            for k in range(2):
                sp.wait_ge(s_gst[k], (NT + 1 - k) // 2 * 16 + 16)
                sp.wait_ge(s_ost[k], (NT + 1 - k) // 2 * 16 + 16)

        @block.gpsimd
        def _(pool):
            G = nc.gpsimd
            G.memset(src_i, PAD_KEY).then_inc(s_pad, 1)
            G.memset(dst_i, PAD_KEY).then_inc(s_pad, 1)
            G.memset(next_i, PAD_KEY).then_inc(s_pad, 1)
            G.memset(typ_i, 0).then_inc(s_pad, 1)
            G.memset(ones[:, :], 1.0).then_inc(s_ones, 1)
            G.memset(ident[:, :], 0.0).then_inc(s_ones, 1)
            G.memset(neg_half[:, :], -0.5).then_inc(s_const, 1)
            G.iota(iota[:, :], pattern=[[1, J]], base=0, channel_multiplier=0,
                   allow_small_or_imprecise_dtypes=True).then_inc(s_const, 1)
            G.iota(iota_p[:, :], pattern=[[0, 1]], base=0, channel_multiplier=1,
                   allow_small_or_imprecise_dtypes=True).then_inc(s_const, 1)
            G.iota(iota_bf[:, :], pattern=[[1, P]], base=0, channel_multiplier=0,
                   allow_small_or_imprecise_dtypes=True).then_inc(s_const, 1)
            pool.wait_ge(s_ones, 2)
            G.affine_select(out=ident[:, :], in_=ident[:, :], compare_op=ALU.not_equal, fill=1.0,
                            base=0, pattern=[[-1, P]], channel_multiplier=1).then_inc(s_const, 1)
            G.affine_select(out=before, in_=ones[:, :], compare_op=ALU.is_ge, fill=0.0,
                            base=-1, pattern=[[1, P]], channel_multiplier=-1).then_inc(s_const, 1)

            def scatter(n, issue_more=None):
                flat = pays[n].rearrange("p c w -> p (c w)")

                def issue(i):
                    for h in range(2):
                        at = i * (2 * H) + h * H
                        if not (isinstance(i, int) and i == 0):
                            for k in range(h * H, h * H + H):
                                pool.wait_ge(s_slot[n][k], i * 16)
                            pool.sem_inc(s_go, 1)
                        G.tensor_copy(stage_i[:, h, :], pos_is[n][:, bass.ds(at, H)]).then_inc(s_stage[n], 1)
                        G.tensor_copy(stage_v[:, h].rearrange("p k w -> p (k w)"),
                                      flat[:, bass.ds(at * 2, 2 * H)]).then_inc(s_stage[n], 1)
                        pool.wait_ge(s_stage[n], i * 4 + (2 * h + 2))
                        pool.sem_inc(s_go, 1)
                        for k in range(H):
                            pool.indirect_dma_start(
                                tables[n][:, :], bass.IndirectOffsetOnAxis(ap=stage_i[:, h, k:k + 1], axis=0),
                                stage_v[:, h, k, :], None).then_inc(s_slot[n][h * H + k], 16)

                last = C // (2 * H)
                issue(0)
                if n == 0:
                    with pool.Fori(1, last) as i:
                        issue(i)
                else:
                    with pool.Fori(1, NT + 1) as i:
                        issue(i)
                        root(i)
                    for i in range(NT + 1, last):
                        issue(i)
                for k in range(2 * H):
                    pool.wait_ge(s_slot[n][k], last * 16)

            def root(count):
                pool.wait_ge(s_ve, count)
                G.tensor_tensor(rs[:, :], ve[:, :], neg_half[:, 0:1], ALU.pow).then_inc(s_rs, 1)

            pool.wait_ge(s_flag, 1)
            unsorted = pool.value_load(flag_i[0:1, 0:1], min_val=0, max_val=1)
            pool.wait_ge(s_pos[0], 1)
            with pool.If(unsorted > 0):
                scatter(0)
            with pool.Else():
                pool.dma_start(table0.rearrange("(p c) w -> p (c w)", c=C),
                               pay0.rearrange("p c w -> p (c w)")).then_inc(s_nat, 16)
                pool.wait_ge(s_nat, 16)
            pool.sem_inc(s_table[0], 1)

            def gather(n, source):
                for _ in range(S):
                    pool.sem_inc(s_free[n], 1)
                pool.wait_ge(s_plan_rd, n + 1)
                with pool.Fori(0, NG // S) as i:
                    for s in range(S):
                        pool.wait_ge(s_free[n], i * S + (s + 1))
                        pool.sem_inc(s_go, 1)
                        G.tensor_copy(ids[:, s, :], tidx[:, bass.ds(i * (S * H) + s * H, H)]).then_inc(s_ids[n], 1)
                        pool.wait_ge(s_ids[n], i * S + (s + 1))
                        pool.sem_inc(s_go, 1)
                        for k in range(H):
                            pool.indirect_dma_start(
                                rows[:, (s * H + k) * D:(s * H + k + 1) * D], None, source,
                                bass.IndirectOffsetOnAxis(ap=ids[:, s, k:k + 1], axis=0)
                            ).then_inc(s_rows[s * H + k], 16)

            gather(0, x[:, :])
            pool.wait_ge(s_deg1, 1)
            G.tensor_tensor(deg_rs[:, :], deg_rs[:, :], neg_half[:, :], ALU.pow).then_inc(s_degr, 1)
            pool.wait_ge(s_pos[1], 1)
            scatter(1)
            pool.sem_inc(s_table[1], 1)
            for k in range(2):
                pool.wait_ge(s_gst[k], (NT + 1 - k) // 2 * 16 + 16)
            gather(1, gdram[:, :])
            with pool.Fori(NT + 1, 2 * NT + 1) as t:
                root(t)

        @block.vector
        def _(dve):
            V = nc.vector
            own, sort = Count(s_v), Count(s_sort)
            order = [own]

            def note(ins):
                order[0].add(ins)

            def settle():
                dve.wait_ge(order[0].sem, order[0].value())

            def step(ins):
                note(ins)
                settle()

            def rounded(out_ap, in_ap, shift, scale):
                step(V.tensor_scalar(out_ap, in_ap, shift, scale, ALU.add, ALU.mult))
                step(V.tensor_scalar(out_ap, out_ap, MAGIC, None, ALU.add))
                step(V.tensor_scalar(out_ap, out_ap, MAGIC, None, ALU.subtract))

            def floor_of(out_ap, in_ap, unit):
                rounded(out_ap, in_ap, -(unit - 1) / 2, 1.0 / unit)

            def prepare(n):
                key, val = ((dst_i, src_i), (src_i, dst_i))[n]
                lo = lo1 if n else pos
                step(V.tensor_copy(lo, key))
                note(V.tensor_copy(pays[n][:, :, 1], lo))
                step(V.tensor_copy(scan, val))
                step(V.tensor_scalar(mask, scan, float(PAD_KEY), None, ALU.is_lt))
                step(V.tensor_tensor(scan, scan, mask, ALU.mult))
                if n == 0:
                    step(V.tensor_copy(mask, typ_i))
                    step(V.scalar_tensor_tensor(pay0[:, :, 0], scan, float(R), mask, ALU.mult, ALU.add))
                else:
                    step(V.tensor_scalar(pay1[:, :, 0], scan, float(R), None, ALU.mult))
                floor_of(his[n], lo, P)
                if n:
                    step(V.scalar_tensor_tensor(lo1, hi1, -float(P), lo1, ALU.mult, ALU.add))

            def count(n):
                with dve.Fori(0, B) as b:
                    own.enter(b, 1)
                    step(V.tensor_scalar(mask, his[n], iota[:, bass.ds(b, 1)], None, ALU.is_equal, ALU.add,
                                         accum_out=counts[:, n, bass.ds(b, 1)]))
                own.leave(B)
                dve.sem_inc(s_cnt[n], 1)

            def bucket_ends(n):
                row = rowset[:, n]
                dve.wait_ge(s_cnt_mm[n], 1)
                step(V.tensor_copy(row[:, 6, :], ps[:, 2, 0:B]))
                note(V.memset(base[:, B:RANKS], 0.0))
                step(V.memset(row[:, 5, :], 0.0))
                step(V.tensor_tensor_scan(row[:, 0, :], row[:, 6, :], row[:, 5, :], 0.0, ALU.add, ALU.add))
                step(V.tensor_tensor(row[:, 1, :], row[:, 0, :], row[:, 6, :], ALU.subtract))
                step(V.tensor_tensor(base[:, 0:B], row[:, 1, :], ps[:, 3, 0:B], ALU.add))

            def rank_a(n, b):
                step(V.tensor_scalar(mask, his[n], iota[:, bass.ds(b, 1)], None, ALU.is_equal))
                step(V.tensor_tensor_scan(scan, mask, mask, base[:, bass.ds(b, 1)], ALU.add, ALU.max))

            def rank_b():
                step(V.tensor_tensor(scan, scan, mask, ALU.mult))
                step(V.tensor_tensor(pos, pos, scan, ALU.add))

            def plan(n, width):
                row = rowset[:, n]
                floor_of(row[:, 2, :], row[:, 1, :], H * P)
                step(V.tensor_scalar(row[:, 1, :], row[:, 0, :], 1.0, None, ALU.subtract))
                floor_of(row[:, 3, :], row[:, 1, :], H * P)
                step(V.tensor_tensor(row[:, 3, :], row[:, 3, :], row[:, 2, :], ALU.subtract))
                step(V.tensor_scalar(row[:, 3, :], row[:, 3, :], 1.0, 1.0, ALU.add, ALU.max))
                step(V.tensor_tensor_scan(row[:, 4, :], row[:, 3, :], row[:, 5, :], 0.0, ALU.add, ALU.add))
                step(V.tensor_tensor(row[:, 3, :], row[:, 3, :], row[:, 4, :], ALU.subtract))
                step(V.tensor_tensor(row[:, 3, :], row[:, 3, :], row[:, 2, :], ALU.add))
                step(V.memset(row[:, 2, :], 0.0))
                step(V.tensor_tensor(row[:, 2, 0:NT - 1], row[:, 3, 1:NT], row[:, 3, 0:NT - 1], ALU.subtract))
                for c, r in ((0, 4), (1, 2)):
                    step(V.tensor_tensor(row[0:NT, 7, 0:NT], row[0:NT, r, 0:NT], ident[0:NT, 0:NT], ALU.mult))
                    step(V.reduce_sum(col[0:NT, c:c + 1], row[0:NT, 7, 0:NT], axis=AX_X))
                note(V.tensor_scalar(past[0:NT, :], iota[0:NT, 0:J], col[0:NT, 0:1], None, ALU.is_ge))
                step(V.tensor_scalar(colrep[0:NT, :], ones[0:NT, :], col[0:NT, 1:2], None, ALU.mult))
                dve.sem_inc(s_past, 1)
                dve.wait_ge(s_plan_mm, n + 1)
                note(V.tensor_copy(node_t[:, :], ps[:, 2, 0:J]))
                note(V.tensor_scalar(node_p[:, 0:J], ps[:, 2, 0:J], float(P), None, ALU.mult))
                step(V.tensor_tensor(grp_t[:, :], ps[:, 3, 0:J], iota[:, 0:J], ALU.add))
                step(V.tensor_scalar(grp_t[:, :], grp_t[:, :], float(NG - 1), None, ALU.min))
                step(V.tensor_scalar(past[:, :], grp_t[:, :], iota_p[:, 0:1], None, ALU.is_le))
                step(V.reduce_sum(upto[:, :], past[:, :], axis=AX_X))
                dve.sem_inc(s_upto, 1)
                floor_of(grp_m[:, :], grp_t[:, :], S)
                step(V.scalar_tensor_tensor(grp_m[:, :], grp_m[:, :], -float(S), grp_t[:, :], ALU.mult, ALU.add))
                note(V.tensor_scalar(steps_i[0:1, 0:J, 0], node_t[0:1, :], float(width), None, ALU.mult))
                note(V.tensor_scalar(steps_i[0:1, 0:J, 1], grp_t[0:1, :], float(H), None, ALU.mult))
                note(V.tensor_scalar(steps_i[0:1, 0:J, 2], grp_m[0:1, :], float(H * D), None, ALU.mult))
                note(V.tensor_scalar(steps_i[0:1, 0:J, 3], grp_t[0:1, :], 1.0, None, ALU.add))
                dve.wait_ge(s_upto_mm, n + 1)
                note(V.tensor_copy(free_i[0:1, :], ps[0:1, 2, 0:P]))
                dve.wait_ge(s_exp, n + 1)
                for c, (a, z) in enumerate(((0, 512), (512, C))):
                    note(V.tensor_copy(ttyp[:, a:z], ps[:, 4 + c, 0:z - a]))
                    note(V.tensor_copy(tkey[:, a:z], ps[:, 6 + c, 0:z - a]))
                settle()
                rounded(tbuf, ttyp[:, :], -7.5, 1.0 / R)
                note(V.tensor_copy(tidx[:, :], tbuf))
                step(V.scalar_tensor_tensor(ttyp[:, :], tbuf, -float(R), ttyp[:, :], ALU.mult, ALU.add))
                dve.sem_inc(s_plan_rd, 1)

            def one_hot(out_ap, numbers, keys, width):
                return V.tensor_tensor(
                    out_ap, numbers[:, 0:width].rearrange("p (a v) -> p a v", a=1).to_broadcast([P, H, width]),
                    keys.rearrange("p (k a) -> p k a", a=1).to_broadcast([P, H, width]), ALU.is_equal)

            def hots(n, j, h, tiles):
                V.tensor_scalar(klo[:, h, :], tkey[:, bass.ds(tiles, H)], node_p[:, bass.ds(j, 1)], None,
                                ALU.subtract).then_inc(s_klo[n], 1)
                dve.wait_ge(s_klo[n], j + 1)
                one_hot(onehot[:, h], iota, klo[:, h, :], P).then_inc(s_oh[n], 1)
                if n == 0:
                    one_hot(onetyp[:, h], iota, ttyp[:, bass.ds(tiles, H)], R).then_inc(s_oh[n], 1)

            def walk(n, sums, width, first, last, beside=None, noted=0):
                if first == 0:
                    dve.sem_inc(s_acc[n], 2)
                    hots(n, 0, 0, dve.value_load(steps_v[0:1, 1:2], min_val=0, max_val=C - H))
                before_loop = own.value()
                with dve.Fori(first // 2, last // 2) as i:
                    if noted:
                        own.base, own.k = (i - first // 2) * noted + before_loop, 0
                    for h in range(2):
                        j = i * 2 + h
                        at = dve.value_load(steps_v[0:1, bass.ds(j * 4, 1)], min_val=0, max_val=NT * width)
                        tiles = dve.value_load(steps_v[0:1, bass.ds(j * 4 + 5, 1)], min_val=0, max_val=C - H)
                        hots(n, j + 1, 1 - h, tiles)
                        if beside:
                            beside(i, h)
                        dve.wait_ge(s_mm[n], j + 1)
                        dve.wait_ge(s_acc[n], j + 2)
                        dest = sums[:, bass.ds(at, width)]
                        V.tensor_tensor(dest, dest, ps[:, h, 0:width], ALU.add).then_inc(s_acc[n], 1)
                if noted:
                    assert own.k == noted
                    own.base, own.k = before_loop + (last - first) // 2 * noted, 0

            def ranks_and_degrees(i, h):
                j = i * 2 + h
                dve.wait_ge(s_deg_mm, j + 1)
                for out_ap, keys, width in ((oh_lo[:, h], lo1, P), (oh_hi[:, h], hi1, NT)):
                    one_hot(out_ap, iota_bf, keys[:, bass.ds(j * H, H)], width).then_inc(s_deg_oh, 1)
                if h == 0:
                    rank_a(1, i)
                else:
                    rank_b()

            def moments(value):
                step(V.bn_stats(st[:, :], y[:, :]))
                dve.sem_inc(s_vgo, 1)
                step(V.bn_aggr(mv[:, :], st[:, :]))
                V.tensor_scalar(ve[:, :], mv[:, 1:2], EPS, None, ALU.add).then_inc(s_ve, 1)
                dve.wait_ge(s_rs, value)

            def gru(t, k):
                dve.wait_ge(s_rkrel, t + 1)
                V.tensor_copy(red[:, :], sums0[:, bass.ds(t * W0, W0)]).then_inc(s_redr, 1)
                dve.wait_ge(s_gates, t + 2)
                V.tensor_tensor(gate[:, :], ps[:, 2, :], bias[:, 0:2 * D], ALU.add).then_inc(s_rz, 1)
                note(V.tensor_tensor(tA[:, :], ps[:, 3, 0:D], bias[:, 2 * D:3 * D], ALU.add))
                note(V.tensor_tensor(hn[:, :], ps[:, 3, D:2 * D], bias[:, 3 * D:4 * D], ALU.add))
                settle()
                dve.wait_ge(s_rzs, t + 1)
                step(V.scalar_tensor_tensor(tB[:, :], gate[:, 0:D], 1.0, hn[:, :], ALU.add, ALU.mult))
                V.scalar_tensor_tensor(tA[:, :], tB[:, :], 0.5, tA[:, :], ALU.mult, ALU.add).then_inc(s_npre, 1)
                dve.wait_ge(s_n, t + 1)
                step(V.tensor_tensor(y[:, :], xt[:, k, :], tB[:, :], ALU.subtract))
                step(V.scalar_tensor_tensor(y[:, :], gate[:, D:2 * D], 1.0, y[:, :], ALU.add, ALU.mult))
                step(V.scalar_tensor_tensor(y[:, :], y[:, :], 0.5, tB[:, :], ALU.mult, ALU.add))
                step(V.tensor_tensor(y[:, :], y[:, :], xt[:, k, :], ALU.add))
                moments(t + 1)
                note(V.tensor_scalar(sums0[:, bass.ds(t * W0, D)], y[:, :], mv[:, 0:1], rs[:, :],
                                     ALU.subtract, ALU.mult))
                dve.wait_ge(s_x1tr, t + 1)
                V.tensor_scalar(x1c[:, :], y[:, :], mv[:, 0:1], rs[:, :], ALU.subtract, ALU.mult).then_inc(s_x1, 1)
            GRU_STEPS = 10

            def put_g(t, stored, k):
                dve.wait_ge(s_h, t + 2)
                note(V.tensor_scalar(sums1[:, bass.ds(t * D, D)], ps[:, 5, 0:D], deg_rs[:, bass.ds(t, 1)], None,
                                     ALU.mult))
                dve.wait_ge(s_gst[k], stored * 16 + 16)
                V.tensor_scalar(gt[:, k, :], ps[:, 5, 0:D], deg_rs[:, bass.ds(t, 1)], None,
                                ALU.mult).then_inc(s_g, 1)

            def finish(t, stored, k):
                step(V.scalar_tensor_tensor(y[:, :], sums1[:, bass.ds(t * D, D)], deg_rs[:, bass.ds(t, 1)],
                                            sums0[:, bass.ds(t * W0, D)], ALU.mult, ALU.add))
                moments(t + (NT + 1))
                dve.wait_ge(s_ost[k], stored * 16 + 16)
                V.tensor_scalar(ot[:, k, :], y[:, :], mv[:, 0:1], rs[:, :], ALU.subtract, ALU.mult).then_inc(s_o, 1)
                dve.wait_ge(s_o, t + 1)
            FINISH_STEPS = 3

            V.memset(zero_bf[:, :], 0.0).then_inc(s_zero, 1)
            note(V.memset(steps_i[:, :, :], 0))
            step(V.memset(node_p[:, J:J + 2], 0.0))
            dve.sem_inc(s_npre, 1)
            dve.sem_inc(s_g, 1)
            dve.wait_ge(s_const, 6)
            dve.wait_ge(s_edges, 128)
            prepare(1)
            count(1)
            note(V.tensor_copy(scan, dst_i))
            step(V.tensor_copy(pos, next_i))
            step(V.tensor_tensor(mask, scan, pos, ALU.is_gt))
            step(V.reduce_sum(flag[:, 0:1], mask, axis=AX_X))
            dve.sem_inc(s_flag_in, 1)
            prepare(0)
            count(0)
            dve.wait_ge(s_flag_mm, 1)
            step(V.tensor_scalar(flag_i[0:1, :], ps[0:1, 1, 0:1], 0.0, None, ALU.is_gt))
            dve.sem_inc(s_flag, 1)
            bucket_ends(0)
            unsorted = dve.value_load(flag_i[0:1, 0:1], min_val=0, max_val=1)
            with dve.If(unsorted > 0):
                order[0] = sort
                step(V.memset(pos, -1.0))
                with dve.Fori(0, B) as b:
                    sort.enter(b, 4)
                    rank_a(0, b)
                    rank_b()
                sort.leave(B)
                step(V.tensor_copy(pos_is[0], pos))
                order[0] = own
            dve.sem_inc(s_pos[0], 1)
            plan(0, W0)
            bucket_ends(1)
            dve.wait_ge(s_wtr, 28)
            note(V.memset(sums0[:, :], 0.0))
            note(V.memset(sums1[:, NT * D:B * D], 0.0))
            step(V.memset(pos, -1.0))
            dve.sem_inc(s_deg_mm, 2)
            walk(0, sums0, W0, 0, 2 * RANKS, ranks_and_degrees, 4)
            step(V.tensor_copy(pos_is[1], pos))
            dve.sem_inc(s_pos[1], 1)
            dve.wait_ge(s_deg_mm, NG + 3)
            V.tensor_scalar(deg_rs[:, :], ps[:, 7, 0:NT], 1.0, None, ALU.add).then_inc(s_deg1, 1)
            walk(0, sums0, W0, 2 * RANKS, J)
            dve.wait_ge(s_acc[0], J + 2)
            dve.wait_ge(s_degr, 1)
            dve.wait_ge(s_bias, 3)
            gru(0, 0)
            with dve.Fori(0, NT // 2) as i:
                own.enter(i, 2 * (GRU_STEPS + 1))
                for k in range(2):
                    gru(i * 2 + (k + 1), 1 - k)
                    put_g(i * 2 + k, i, k)
            own.leave(NT // 2)
            put_g(NT - 1, NT // 2, 0)
            settle()
            plan(1, D)
            walk(1, sums1, D, 0, J)
            dve.wait_ge(s_acc[1], J + 2)
            with dve.Fori(0, NT // 2) as i:
                own.enter(i, 2 * FINISH_STEPS)
                for k in range(2):
                    finish(i * 2 + k, i, k)
            own.leave(NT // 2)
            finish(NT - 1, NT // 2, 0)

        @block.scalar
        def _(act):
            A = nc.scalar
            act.sem_inc(s_cnT, 1)
            act.sem_inc(s_redt, 1)
            act.sem_inc(s_x1T, 1)
            act.sem_inc(s_wcp, 4)
            at = 0
            for dest in weight_tiles():
                act.wait_ge(s_wtr, at + 1)
                A.copy(dest, ps[:, 4 + at % 4, 0:P]).then_inc(s_wcp, 1)
                at += 1
            for m, (bank, first, size) in enumerate(((4, 0, 2 * D), (5, 2 * D, D), (6, 3 * D, D))):
                act.wait_ge(s_bias_mm, m + 1)
                A.copy(bias[:, first:first + size], ps[:, bank, 0:size]).then_inc(s_bias, 1)

            def front(t):
                act.wait_ge(s_xtr, t + 1)
                act.wait_ge(s_gates, t + 1)
                A.copy(xT[:, :], ps[:, 0, 0:D]).then_inc(s_xT, 1)
                A.copy(cnT[:, :], ps[0:R, 0, D:D + P]).then_inc(s_cnT, 1)
                act.wait_ge(s_rkrel, t + 2)
                A.copy(redT[:, :], ps[:, 1, 0:D]).then_inc(s_redt, 1)
                act.wait_ge(s_rz, t + 1)
                A.activation(gate[:, :], gate[:, :], ACT.Tanh, scale=0.5).then_inc(s_rzs, 1)
                act.wait_ge(s_npre, t + 2)
                A.activation(tB[:, :], tA[:, :], ACT.Tanh).then_inc(s_n, 1)

            def back(t):
                act.wait_ge(s_x1tr, t + 2)
                act.wait_ge(s_h, t + 1)
                A.copy(x1T[:, :], ps[:, 4, 0:D]).then_inc(s_x1T, 1)

            def arrivals(n):
                with act.Fori(0, NG // S) as i:
                    for s in range(S):
                        for k in range(H):
                            act.wait_ge(s_rows[s * H + k], i * 16 + (n * NG // S * 16 + 16))
                        act.sem_inc(s_grp[n], 1)

            arrivals(0)
            front(0)
            with act.Fori(0, NT // 2) as i:
                for k in range(2):
                    front(i * 2 + (k + 1))
                    back(i * 2 + k)
            back(NT - 1)
            arrivals(1)

        @block.tensor
        def _(pe):
            M = nc.tensor
            pe.sem_inc(s_gates, 1)
            pe.sem_inc(s_x1tr, 1)
            pe.sem_inc(s_h, 1)
            pe.sem_inc(s_rkrel, 1)
            pe.wait_ge(s_const, 6)
            pe.wait_ge(s_w, 64)
            blocks = [wnat[:, a, k, c * P:(c + 1) * P] for a in range(2) for k in range(G3 // P) for c in range(2)]
            blocks += [w1nat[:, k, c * P:(c + 1) * P] for k in range(2) for c in range(2)]
            for at, b in enumerate(blocks):
                pe.wait_ge(s_wcp, at + 1)
                M.transpose(ps[:, 4 + at % 4, 0:P], b, ident[:, :]).then_inc(s_wtr, 1)
            pe.wait_ge(s_wcp, len(blocks) + 4)
            pe.wait_ge(s_brow, 32)
            one = ones[0:1, :]
            M.matmul(ps[:, 4, :], one, brow[0:1, 0:2 * D], start=True, stop=False)
            M.matmul(ps[:, 4, :], one, brow[0:1, G3:G3 + 2 * D], start=False, stop=True).then_inc(s_bias_mm, 1)
            M.matmul(ps[:, 5, 0:D], one, brow[0:1, 2 * D:G3], start=True, stop=True).then_inc(s_bias_mm, 1)
            M.matmul(ps[:, 6, 0:D], one, brow[0:1, G3 + 2 * D:2 * G3], start=True, stop=True).then_inc(s_bias_mm, 1)
            pe.wait_ge(s_flag_in, 1)
            M.matmul(ps[:, 1, 0:1], ones[:, :], flag[:, 0:1], start=True, stop=True).then_inc(s_flag_mm, 1)

            def count(n):
                pe.wait_ge(s_cnt[n], 1)
                M.matmul(ps[:, 2, 0:B], ones[:, :], counts[:, n, :], start=True, stop=True)
                M.matmul(ps[:, 3, 0:B], before, counts[:, n, :], start=True, stop=True).then_inc(s_cnt_mm[n], 1)

            def plan(n):
                pe.wait_ge(s_past, n + 1)
                M.matmul(ps[:, 2, 0:J], ones[0:NT, :], past[0:NT, :], start=True, stop=True)
                M.matmul(ps[:, 3, 0:J], colrep[0:NT, :], past[0:NT, :], start=True, stop=True).then_inc(s_plan_mm, 1)
                pe.wait_ge(s_upto, n + 1)
                M.matmul(ps[0:1, 2, 0:P], upto[:, 0:1], ident[:, :], start=True, stop=True).then_inc(s_upto_mm, 1)
                pe.wait_ge(s_chunk, 16 * KC * (n + 1))
                pe.wait_ge(s_bias, 3)
                for w in range(2):
                    for k, r in enumerate(KROWS):
                        bank, a = 4 + 2 * w + k * P // 512, k * P % 512
                        last = M.matmul(ps[:, bank, a:a + r], chunk[0:r, k, :, w], ident[0:r, 0:r],
                                        start=True, stop=True)
                last.then_inc(s_exp, 1)

            def walk(n, first, last, beside=None):
                with pe.Fori(first // 2, last // 2) as i:
                    for h in range(2):
                        j = i * 2 + h
                        at = pe.value_load(steps_v[0:1, bass.ds(j * 4 + 2, 1)], min_val=0, max_val=(S - 1) * H * D)
                        group = pe.value_load(steps_v[0:1, bass.ds(j * 4 + 3, 1)], min_val=1, max_val=NG)
                        pe.wait_ge(s_acc[n], j + 1)
                        pe.wait_ge(s_oh[n], (j + 1) * (2 - n))
                        pe.wait_ge(s_grp[n], group)
                        for k in range(H):
                            prod = M.matmul(ps[:, h, 0:D], onehot[:, h, k, :], rows[:, bass.ds(at + k * D, D)],
                                            start=(k == 0), stop=(k == H - 1))
                        if n == 0:
                            for k in range(H):
                                prod = M.matmul(ps[:, h, D:W0], onehot[:, h, k, :], onetyp[:, h, k, :],
                                                start=(k == 0), stop=(k == H - 1))
                        prod.then_inc(s_mm[n], 1)
                        if beside:
                            beside(j, h)

            def degrees(j, h):
                pe.wait_ge(s_deg_oh, (j + 1) * 2)
                for k in range(H):
                    cnt = M.matmul(ps[:, 7, 0:NT], oh_lo[:, h, k, :], oh_hi[:, h, k, :], start=False, stop=False)
                cnt.then_inc(s_deg_mm, 1)

            def front(t, loaded, k):
                pe.wait_ge(s_x[k], loaded * 16 + 16)
                pe.wait_ge(s_redr, t + 1)
                pe.wait_ge(s_cnT, t + 1)
                for c in range(2):
                    M.transpose(ps[:, 0, c * P:c * P + P], xt[:, k, c * P:c * P + P], ident[:, :])
                M.transpose(ps[0:R, 0, D:D + P], red[:, D:W0], ident[:, :]).then_inc(s_xtr, 1)
                pe.wait_ge(s_cnT, t + 2)
                pe.wait_ge(s_redt, t + 1)
                for c in range(2):
                    M.matmul(ps[:, 1, c * P:c * P + P], red[:, c * P:c * P + P], ident[:, :], start=True, stop=False)
                    last = M.matmul(ps[:, 1, c * P:c * P + P], rel_s[:, c * P:c * P + P], cnT[:, :],
                                    start=False, stop=True)
                last.then_inc(s_rkrel, 1)
                pe.wait_ge(s_npre, t + 1)
                pe.wait_ge(s_redt, t + 2)
                parts = [(m[:, c * P:c * P + P], wT[:, a, c, :]) for a, m in ((1, xT), (0, redT)) for c in range(2)]
                for q, (lhs, w) in enumerate(parts):
                    M.matmul(ps[:, 2, :], lhs, w[:, 0:2 * D], start=(q == 0), stop=(q == 3))
                for a, cols in ((1, slice(D, 2 * D)), (0, slice(0, D))):
                    for c in range(2):
                        lhs, w = parts[(1 - a) * 2 + c]
                        last = M.matmul(ps[:, 3, cols], lhs, w[:, 2 * D:G3], start=(c == 0), stop=(c == 1))
                last.then_inc(s_gates, 1)

            def back(t):
                pe.wait_ge(s_x1, t + 1)
                pe.wait_ge(s_x1T, t + 1)
                for c in range(2):
                    last = M.transpose(ps[:, 4, c * P:c * P + P], x1c[:, c * P:c * P + P], ident[:, :])
                last.then_inc(s_x1tr, 1)
                pe.wait_ge(s_g, t + 1)
                pe.wait_ge(s_x1T, t + 2)
                for c in range(2):
                    last = M.matmul(ps[:, 5, 0:D], x1T[:, c * P:c * P + P], w1T[:, c, :], start=(c == 0), stop=(c == 1))
                last.then_inc(s_h, 1)

            count(0)
            plan(0)
            pe.wait_ge(s_plan_rd, 1)
            count(1)
            pe.wait_ge(s_zero, 1)
            M.matmul(ps[:, 7, 0:NT], zero_bf[:, :], zero_bf[:, 0:NT], start=True, stop=False)
            walk(0, 0, 2 * RANKS, degrees)
            M.matmul(ps[:, 7, 0:NT], zero_bf[:, :], zero_bf[:, 0:NT], start=False, stop=True).then_inc(s_deg_mm, 1)
            walk(0, 2 * RANKS, J)
            front(0, 0, 0)
            with pe.Fori(0, NT // 2) as i:
                for k in range(2):
                    front(i * 2 + (k + 1), i + k, 1 - k)
                    back(i * 2 + k)
            back(NT - 1)
            plan(1)
            pe.wait_ge(s_plan_rd, 2)
            walk(1, 0, J)


_INS = ['x', 'src', 'dst', 'edge_type_16', 'L0_gnn_relvectors', 'L0_gnn_w_ih', 'L0_gnn_w_hh', 'L0_gnn_b_ih',
        'L0_gnn_b_hh', 'L1_gnn_W']


def kernel(**inputs):
    import numpy as _np
    import concourse.bacc as _bacc
    from concourse import mybir as _mybir
    from concourse.bass_utils import run_bass_kernel_spmd as _run

    nc = _bacc.Bacc("TRN2", target_bir_lowering=False, num_devices=1)
    arrays, args = {}, []
    for name in _INS:
        a = _np.ascontiguousarray(inputs[name])
        arrays[f"in_{name}_dram"] = a
        args.append(nc.dram_tensor(f"in_{name}_dram", a.shape, _mybir.dt.from_np(a.dtype), kind="ExternalInput").ap())
    f32 = _mybir.dt.float32
    args.append(nc.dram_tensor("out_0_dram", (N, D), f32, kind="ExternalOutput").ap())
    for name, shape in (("table0", (C * P, 2)), ("table1", (C * P, 2)), ("gdram", (N, D))):
        args.append(nc.dram_tensor(name, shape, f32, kind="Internal").ap())
    build(nc, *args)
    r = _run(nc, [arrays], core_ids=[0])
    return r.results[0]["out_0_dram"]
```

```python
from contextlib import ExitStack

import concourse.bass as bass
from concourse import mybir

F32, BF16, I32 = mybir.dt.float32, mybir.dt.bfloat16, mybir.dt.int32
ALU, ACT = mybir.AluOpType, mybir.ActivationFunctionType
AX_X = mybir.AxisListType.X

N, D, E, R = 6250, 256, 106250, 16
P = 128
NT = -(-N // P)
LAST = N - (NT - 1) * P
B = NT + 1
C = 832
PAD_KEY = NT * P
REAL_P = E // C
REAL_C = E - REAL_P * C
H = 8
NG = C // H
J = NG + NT - 1
S = 4
SC = 2 * H
KC = -(-C // P)
KROWS = [min(P, C - k * P) for k in range(KC)]
W0 = D + R
FG = 7
RANKS = NG // 2
U = 4
G3 = 3 * D
MAGIC = 1.5 * 2.0 ** 23
EPS = 1e-5
assert NT % 2 == 1 and NT % FG == 0 and NG % (2 * S) == 0 and C % (2 * SC) == 0 and U == 4 and J % U == 0 and 2 * RANKS % U == 0 and 2 * RANKS == NG and C * P >= E and C % (S * H) == 0 and B <= RANKS


class Count:

    def __init__(self, sem):
        self.sem, self.base, self.k = sem, 0, 0

    def value(self):
        return self.base + self.k

    def add(self, ins):
        ins.then_inc(self.sem, 1)
        self.k += 1

    def enter(self, i, per):
        self.first, self.per = self.value(), per
        self.base, self.k = i * per + self.first, 0

    def leave(self, trips):
        assert self.k == self.per, self.k
        self.base, self.k = self.first + trips * self.per, 0


def build(nc, x, src, dst, etype, rel, w_ih, w_hh, b_ih, b_hh, w1, out, table0, table1, gdram):
    ctx = ExitStack()
    with ctx:
        def sb(name, shape, dt=F32):
            return ctx.enter_context(nc.sbuf_tensor(name, shape, dt))

        def sem(name):
            return ctx.enter_context(nc.semaphore(name))

        ps = ctx.enter_context(nc.psum_tensor("ps", [P, 8, 512], F32))

        iota = sb("iota", [P, J])
        iota_p = sb("iota_p", [P, 1])
        iota_bf = sb("iota_bf", [P, P], BF16)
        ident = sb("ident", [P, P])
        ones = sb("ones", [P, P])
        neg_half = sb("neg_half", [P, NT])
        zero_bf = sb("zero_bf", [P, P], BF16)
        sums1 = sb("sums1", [P, B * D])
        taken = [0]

        def early(*shape, dt=F32):
            size = 1
            for d in shape:
                size *= d
            words = size * (2 if dt == BF16 else 4) // 4
            part = sums1[:, taken[0]:taken[0] + words]
            taken[0] += words
            assert taken[0] <= NT * D
            part = part if dt == F32 else part.bitcast(dt)
            if len(shape) == 2:
                part = part.rearrange("p (a b) -> p a b", a=shape[0])
            if len(shape) == 3:
                part = part.rearrange("p (a b c) -> p a b c", a=shape[0], b=shape[1])
            return part

        src_i = early(C, dt=I32)
        dst_i = early(C, dt=I32)
        typ_i = early(C, dt=I32)
        hi1 = early(C)
        lo1 = early(C)
        mask = early(C)
        scan = early(C)
        pos = early(C)
        pay1 = sb("pay1", [P, C, 2])[:, :, :]
        pos1_i = sb("pos1_i", [P, C], I32)[:, :]
        pos_is = (typ_i, pos1_i)
        stage_i = sb("stage_i", [P, 2, SC], I32)
        stage_v = sb("stage_v", [P, 2, SC, 2])
        oh_lo = early(2, H, P, dt=BF16)
        oh_hi = early(2, H, NT, dt=BF16)
        before = early(P)
        sides = early(C)
        signs = early(B + 1)
        past_by = early(B)
        counts = sb("counts", [P, 2, B])
        flag = sb("flag", [P, 1])
        flag_i = sb("flag_i", [P, 1], I32)
        deg_rs = sb("deg_rs", [P, NT])
        rows = sb("rows", [P, S * H * D])
        chunk = rows[:, 0:KC * P * 2].rearrange("p (k s w) -> p k s w", k=KC, w=2)
        at0 = KC * P * 2
        pay0 = rows[:, at0:at0 + 2 * C].rearrange("p (c w) -> p c w", w=2)
        hi0 = rows[:, at0 + 2 * C:at0 + 3 * C]
        next_i = rows[:, at0 + 3 * C:at0 + 4 * C].bitcast(I32)
        brow = rows[0:1, at0 + 4 * C:at0 + 4 * C + 2 * G3]
        his, pays = (hi0, hi1), (pay0, pay1)
        rowset = sb("rowset", [P, 2, 8, B])
        base = sb("base", [P, RANKS])
        col = sb("col", [P, 2])
        colrep = sb("colrep", [P, P])
        past = sb("past", [P, J])
        node_t = sb("node_t", [P, J])
        node_p = sb("node_p", [P, J + 2])
        grp_t = sb("grp_t", [P, J])
        grp_m = sb("grp_m", [P, J])
        upto = sb("upto", [P, 1])
        steps_i = sb("steps_i", [1, J + 2, 4], I32)
        steps_v = steps_i[:, :, :].rearrange("p j w -> p (j w)")
        tbuf = rows[:, at0:at0 + C]
        free_i = sb("free_i", [1, P], I32)
        tkey = sb("tkey", [P, C])
        tidx = sb("tidx", [P, C + S * H], I32)
        ttyp = sb("ttyp", [P, C])
        ids = sb("ids", [P, 2, S * H], I32)
        klo = sb("klo", [P, U, H])
        onehot = sb("onehot", [P, U, H, P])
        onetyp = sb("onetyp", [P, U, H, R])
        sums0 = sb("sums0", [P, B * W0])
        wT = sb("wT", [P, 2, 2, G3])
        w1T = sb("w1T", [P, 2, D])
        rel_s = sb("rel_s", [R, D])
        wnat = sums0[:, 0:2 * G3 // P * D].rearrange("p (a k d) -> p a k d", a=2, d=D)
        w1nat = sums0[:, 2 * G3 // P * D:(2 * G3 // P + 2) * D].rearrange("p (k d) -> p k d", d=D)
        bias = sb("bias", [P, 4 * D])
        xt = sb("xt", [P, 2, D])
        xT, redT, tA, tB, hn, y = (rows[:, m * D:m * D + D] for m in range(16, 22))
        gate = rows[:, 22 * D:24 * D]
        red = rows[:, 24 * D:24 * D + W0]
        cnT = rows[0:R, 26 * D:26 * D + P]
        x1c, x1T = rows[:, 28 * D:29 * D], rows[:, 29 * D:30 * D]
        gt = rows[:, 30 * D:32 * D].rearrange("p (k d) -> p k d", k=2)
        st = sb("st", [P, 6])
        mv = sb("mv", [P, 2])
        st_all = rows[:, 0:6 * FG].rearrange("p (t w) -> p t w", w=6)
        mv_all = rows[:, 6 * FG:8 * FG].rearrange("p (t w) -> p t w", w=2)
        ve_all, mean_all, rs_all = (rows[:, m * D:m * D + NT] for m in range(1, 4))
        ve = sb("ve", [P, 1])
        rs = sb("rs", [P, 1])

        def per_layer(name):
            return [sem(f"{name}{n}") for n in range(2)]

        s_const, s_zero, s_pad, s_edges = sem("s_const"), sem("s_zero"), sem("s_pad"), sem("s_edges")
        s_w, s_brow = sem("s_w"), sem("s_brow")
        s_v = sem("s_v")
        s_sort = sem("s_sort")
        s_ones = sem("s_ones")
        s_wtr, s_wcp, s_bias_mm, s_bias = sem("s_wtr"), sem("s_wcp"), sem("s_bias_mm"), sem("s_bias")
        s_flag_in, s_flag_mm, s_flag, s_nat = sem("s_flag_in"), sem("s_flag_mm"), sem("s_flag"), sem("s_nat")
        s_cnt, s_cnt_mm, s_pos, s_stage = map(per_layer, ("s_cnt", "s_cnt_mm", "s_pos", "s_stage"))
        s_hi1, s_sign = sem("s_hi1"), sem("s_sign")
        s_slot = [[sem(f"s_slot{n}_{k}") for k in range(SC)] for n in range(2)]
        s_table = per_layer("s_table")
        s_deg_oh, s_deg_mm, s_deg1, s_degr = sem("s_deg_oh"), sem("s_deg_mm"), sem("s_deg1"), sem("s_degr")
        s_grp, s_free, s_klo = map(per_layer, ("s_grp", "s_free", "s_klo"))
        s_upto, s_upto_mm, s_rkrel, s_cnT = sem("s_upto"), sem("s_upto_mm"), sem("s_rkrel"), sem("s_cnT")
        s_redr, s_redt = sem("s_redr"), sem("s_redt")
        s_chunk, s_past, s_plan_mm, s_plan_rd = sem("s_chunk"), sem("s_past"), sem("s_plan_mm"), sem("s_plan_rd")
        s_exp = sem("s_exp")
        s_rows = [sem(f"s_rows{k}") for k in range(S * H)]
        s_ids, s_oh, s_mm, s_acc = map(per_layer, ("s_ids", "s_oh", "s_mm", "s_acc"))
        s_go = sem("s_go")
        s_vgo = sem("s_vgo")
        s_x, s_gst, s_ost = per_layer("s_xt"), per_layer("s_gst"), sem("s_ost")
        s_var, s_root, s_shift = sem("s_var"), sem("s_root"), sem("s_shift")
        s_xtr, s_xT, s_rel, s_red, s_gates = (sem(n) for n in ("s_xtr", "s_xT", "s_rel", "s_red", "s_gates"))
        s_rz, s_rzs, s_npre, s_n = (sem(n) for n in ("s_rz", "s_rzs", "s_npre", "s_n"))
        s_ve, s_rs = sem("s_ve"), sem("s_rs")
        s_x1, s_x1tr, s_x1T, s_h, s_g, s_o = (sem(n) for n in ("s_x1", "s_x1tr", "s_x1T", "s_h", "s_g", "s_o"))

        tables = (table0, table1)
        def weight_tiles():
            for a in range(2):
                for k in range(G3 // P):
                    for c in range(2):
                        yield wT[:, a, c, k * P:(k + 1) * P]
            for k in range(2):
                for c in range(2):
                    yield w1T[:, c, k * P:(k + 1) * P]

        block = ctx.enter_context(nc.Block())

        @block.sync
        def _(sp):
            for k in range(2):
                sp.sem_inc(s_gst[k], 16)
            for a, w in enumerate((w_ih, w_hh)):
                sp.dma_start(wnat[:, a], w.rearrange("(k p) d -> p k d", p=P)).then_inc(s_w, 16)
            sp.dma_start(w1nat, w1.rearrange("(k p) d -> p k d", p=P)).then_inc(s_w, 16)
            sp.dma_start(rel_s[:, :], rel).then_inc(s_w, 16)
            for a, b in enumerate((b_ih, b_hh)):
                sp.dma_start(brow[0:1, a * G3:(a + 1) * G3], b.rearrange("(a n) -> a n", a=1)).then_inc(s_brow, 16)
            sp.wait_ge(s_pad, 4)
            for t, a, first in ((dst_i, dst, 0), (next_i, dst, 1), (src_i, src, 0), (typ_i, etype, 0)):
                sp.dma_start(t[0:REAL_P, :],
                             a[first:REAL_P * C + first].rearrange("(p c) -> p c", c=C)).then_inc(s_edges, 16)
                sp.dma_start(t[REAL_P:REAL_P + 1, 0:REAL_C - first],
                             a[REAL_P * C + first:E].rearrange("(p c) -> p c", p=1)).then_inc(s_edges, 16)
            def load_table(n):
                sp.wait_ge(s_table[n], 1)
                for k in range(KC):
                    r = KROWS[k]
                    sp.dma_start(chunk[0:r, k].rearrange("t s w -> t (s w)"),
                                 tables[n][k * P * P:(k * P + r) * P, :].rearrange(
                                     "(t s) w -> t (s w)", s=P)).then_inc(s_chunk, 16)

            def free_groups(n):
                sp.wait_ge(s_plan_rd, n + 1)
                with sp.Fori(0, NG) as g:
                    pairs = sp.value_load(free_i[0:1, bass.ds(g, 1)], min_val=1, max_val=J)
                    sp.wait_ge(s_mm[n], pairs)
                    sp.sem_inc(s_free[n], 1)

            def load_x(t, k, rws):
                sp.dma_start(xt[0:rws, k, :], x[bass.ds(t * P, rws), :]).then_inc(s_x[k], 16)

            def store(dest, tile, ready, value, done, t, k, rws):
                sp.wait_ge(ready, value)
                sp.dma_start(dest[bass.ds(t * P, rws), :], tile[0:rws, k, :]).then_inc(done[k], 16)

            load_x(0, 0, P)
            load_x(1, 1, P)
            load_table(0)
            free_groups(0)
            with sp.Fori(0, NT // 2 - 1) as i:
                for k in range(2):
                    t = i * 2 + k
                    sp.wait_ge(s_x1, t + 1)
                    load_x(t + 2, k, P)
                    store(gdram, gt, s_g, t + 2, s_gst, t, k, P)
            sp.wait_ge(s_x1, NT - 2)
            load_x(NT - 1, 0, LAST)
            for t in range(NT - 3, NT):
                store(gdram, gt, s_g, t + 2, s_gst, t, t % 2, P if t < NT - 1 else LAST)
            load_table(1)
            free_groups(1)
            def put(t, tiles, rws):
                sp.wait_ge(s_o, t + tiles)
                sp.dma_start(out[bass.ds(t * P, rws + (tiles - 1) * P), :].rearrange("(s p) d -> p s d", p=rws),
                             sums1[0:rws, bass.ds(t * D, tiles * D)].rearrange("p (s d) -> p s d", d=D)
                             ).then_inc(s_ost, 16)

            with sp.Fori(0, NT // FG - 1) as i:
                put(i * FG, FG, P)
            put(NT - FG, FG - 1, P)
            put(NT - 1, 1, LAST)
            for k in range(2):
                sp.wait_ge(s_gst[k], (NT + 1 - k) // 2 * 16 + 16)
            sp.wait_ge(s_ost, (NT // FG + 1) * 16)

        @block.gpsimd
        def _(pool):
            G = nc.gpsimd
            G.memset(src_i, PAD_KEY).then_inc(s_pad, 1)
            G.memset(dst_i, PAD_KEY).then_inc(s_pad, 1)
            G.memset(next_i, PAD_KEY).then_inc(s_pad, 1)
            G.memset(typ_i, 0).then_inc(s_pad, 1)
            G.memset(tidx[:, C:C + S * H], 0).then_inc(s_ones, 1)
            G.memset(ones[:, :], 1.0).then_inc(s_ones, 1)
            G.memset(ident[:, :], 0.0).then_inc(s_ones, 1)
            G.memset(neg_half[:, :], -0.5).then_inc(s_const, 1)
            G.iota(iota[:, :], pattern=[[1, J]], base=0, channel_multiplier=0,
                   allow_small_or_imprecise_dtypes=True).then_inc(s_const, 1)
            G.iota(iota_p[:, :], pattern=[[0, 1]], base=0, channel_multiplier=1,
                   allow_small_or_imprecise_dtypes=True).then_inc(s_const, 1)
            G.iota(iota_bf[:, :], pattern=[[1, P]], base=0, channel_multiplier=0,
                   allow_small_or_imprecise_dtypes=True).then_inc(s_const, 1)
            pool.wait_ge(s_ones, 3)
            G.affine_select(out=ident[:, :], in_=ident[:, :], compare_op=ALU.not_equal, fill=1.0,
                            base=0, pattern=[[-1, P]], channel_multiplier=1).then_inc(s_const, 1)
            G.affine_select(out=before, in_=ones[:, :], compare_op=ALU.is_ge, fill=0.0,
                            base=-1, pattern=[[1, P]], channel_multiplier=-1).then_inc(s_const, 1)

            def scatter(n):
                flat = pays[n].rearrange("p c w -> p (c w)")

                def stage(i, p):
                    G.tensor_copy(stage_i[:, p, :], pos_is[n][:, bass.ds(i * SC, SC)]).then_inc(s_stage[n], 1)
                    G.tensor_copy(stage_v[:, p].rearrange("p k w -> p (k w)"),
                                  flat[:, bass.ds(i * (2 * SC), 2 * SC)]).then_inc(s_stage[n], 1)

                def issue(i, p, ahead=True):
                    pool.wait_ge(s_stage[n], i * 2 + 2)
                    for half in (range(H), range(H, SC)):
                        if not (isinstance(i, int) and i == 0):
                            for k in half:
                                pool.wait_ge(s_slot[n][k], i * 16)
                        pool.sem_inc(s_go, 1)
                        if half[0] and ahead:
                            stage(i + 1, 1 - p)
                        for k in half:
                            pool.indirect_dma_start(
                                tables[n][:, :], bass.IndirectOffsetOnAxis(ap=stage_i[:, p, k:k + 1], axis=0),
                                stage_v[:, p, k, :], None).then_inc(s_slot[n][k], 16)

                last = C // SC
                looped = last - 2 if n == 0 else NT - 1
                stage(0, 0)
                issue(0, 0)
                if n:
                    pool.wait_ge(s_deg1, 1)
                    G.tensor_tensor(deg_rs[:, :], deg_rs[:, :], neg_half[:, :], ALU.pow).then_inc(s_degr, 1)
                    root(1)
                with pool.Fori(0, looped // 2) as i:
                    for p in range(2):
                        issue(i * 2 + (p + 1), 1 - p)
                        if n:
                            root(i * 2 + (p + 2))
                for q in range(looped + 1, last):
                    issue(q, q % 2, q < last - 1)
                for k in range(SC):
                    pool.wait_ge(s_slot[n][k], last * 16)

            def root(count):
                pool.wait_ge(s_ve, count)
                G.tensor_tensor(rs[:, :], ve[:, :], neg_half[:, 0:1], ALU.pow).then_inc(s_rs, 1)

            pool.wait_ge(s_flag, 1)
            unsorted = pool.value_load(flag_i[0:1, 0:1], min_val=0, max_val=1)
            pool.wait_ge(s_pos[0], 1)
            with pool.If(unsorted > 0):
                scatter(0)
            with pool.Else():
                pool.dma_start(table0.rearrange("(p c) w -> p (c w)", c=C),
                               pay0.rearrange("p c w -> p (c w)")).then_inc(s_nat, 16)
                pool.wait_ge(s_nat, 16)
            pool.sem_inc(s_table[0], 1)

            def gather(n, source):
                def stage(i, p):
                    G.tensor_copy(ids[:, p, :], tidx[:, bass.ds(i * (S * H), S * H)]).then_inc(s_ids[n], 1)

                for _ in range(S):
                    pool.sem_inc(s_free[n], 1)
                pool.wait_ge(s_plan_rd, n + 1)
                stage(0, 0)
                with pool.Fori(0, NG // S // 2) as i:
                    for p in range(2):
                        pool.wait_ge(s_ids[n], i * 2 + (p + 1))
                        for s in range(S):
                            pool.wait_ge(s_free[n], i * (2 * S) + (p * S + s + 1))
                            pool.sem_inc(s_go, 1)
                            if s == S - 1:
                                stage(i * 2 + (p + 1), 1 - p)
                            for k in range(H):
                                pool.indirect_dma_start(
                                    rows[:, (s * H + k) * D:(s * H + k + 1) * D], None, source,
                                    bass.IndirectOffsetOnAxis(ap=ids[:, p, s * H + k:s * H + k + 1], axis=0)
                                ).then_inc(s_rows[s * H + k], 16)

            gather(0, x[:, :])
            pool.wait_ge(s_pos[1], 1)
            scatter(1)
            pool.sem_inc(s_table[1], 1)
            for k in range(2):
                pool.wait_ge(s_gst[k], (NT + 1 - k) // 2 * 16 + 16)
            gather(1, gdram[:, :])
            with pool.Fori(0, NT // FG) as i:
                pool.wait_ge(s_var, i + 1)
                G.tensor_tensor(rs_all[:, bass.ds(i * FG, FG)], ve_all[:, bass.ds(i * FG, FG)],
                                neg_half[:, 0:FG], ALU.pow).then_inc(s_root, 1)

        @block.vector
        def _(dve):
            V = nc.vector
            own, sort = Count(s_v), Count(s_sort)
            order = [own]

            def note(ins):
                order[0].add(ins)

            def settle():
                dve.wait_ge(order[0].sem, order[0].value())

            def step(ins):
                note(ins)
                settle()

            def rounded(out_ap, in_ap, shift, scale):
                step(V.tensor_scalar(out_ap, in_ap, shift, scale, ALU.add, ALU.mult))
                step(V.tensor_scalar(out_ap, out_ap, MAGIC, None, ALU.add))
                step(V.tensor_scalar(out_ap, out_ap, MAGIC, None, ALU.subtract))

            def floor_of(out_ap, in_ap, unit):
                rounded(out_ap, in_ap, -(unit - 1) / 2, 1.0 / unit)

            def prepare(n):
                key, val = ((dst_i, src_i), (src_i, dst_i))[n]
                lo = lo1 if n else pos
                step(V.tensor_copy(lo, key))
                note(V.tensor_copy(pays[n][:, :, 1], lo))
                step(V.tensor_copy(scan, val))
                step(V.tensor_scalar(mask, scan, float(PAD_KEY), None, ALU.is_lt))
                step(V.tensor_tensor(scan, scan, mask, ALU.mult))
                if n == 0:
                    step(V.tensor_copy(mask, typ_i))
                    step(V.scalar_tensor_tensor(pay0[:, :, 0], scan, float(R), mask, ALU.mult, ALU.add))
                else:
                    step(V.tensor_scalar(pay1[:, :, 0], scan, float(R), None, ALU.mult))
                floor_of(his[n], lo, P)
                if n:
                    step(V.scalar_tensor_tensor(lo1, hi1, -float(P), lo1, ALU.mult, ALU.add))

            def count(n):
                with dve.Fori(0, B) as b:
                    own.enter(b, 1)
                    step(V.tensor_scalar(mask, his[n], iota[:, bass.ds(b, 1)], None, ALU.is_equal, ALU.add,
                                         accum_out=counts[:, n, bass.ds(b, 1)]))
                own.leave(B)
                dve.sem_inc(s_cnt[n], 1)

            def bucket_ends(n):
                row = rowset[:, n]
                dve.wait_ge(s_cnt_mm[n], 1)
                step(V.tensor_copy(row[:, 6, :], ps[:, 2, 0:B]))
                note(V.memset(base[:, B:RANKS], 0.0))
                step(V.memset(row[:, 5, :], 0.0))
                step(V.tensor_tensor_scan(row[:, 0, :], row[:, 6, :], row[:, 5, :], 0.0, ALU.add, ALU.add))
                step(V.tensor_tensor(row[:, 1, :], row[:, 0, :], row[:, 6, :], ALU.subtract))
                step(V.tensor_tensor(base[:, 0:B], row[:, 1, :], ps[:, 3, 0:B], ALU.add))

            def rank_a(n, b):
                step(V.tensor_scalar(mask, his[n], iota[:, bass.ds(b, 1)], None, ALU.is_equal))
                step(V.tensor_tensor_scan(scan, mask, mask, base[:, bass.ds(b, 1)], ALU.add, ALU.max))

            def rank_b():
                step(V.tensor_tensor(scan, scan, mask, ALU.mult))
                step(V.tensor_tensor(pos, pos, scan, ALU.add))

            def plan(n, width):
                row = rowset[:, n]
                floor_of(row[:, 2, :], row[:, 1, :], H * P)
                step(V.tensor_scalar(row[:, 1, :], row[:, 0, :], 1.0, None, ALU.subtract))
                floor_of(row[:, 3, :], row[:, 1, :], H * P)
                step(V.tensor_tensor(row[:, 3, :], row[:, 3, :], row[:, 2, :], ALU.subtract))
                step(V.tensor_scalar(row[:, 3, :], row[:, 3, :], 1.0, 1.0, ALU.add, ALU.max))
                step(V.tensor_tensor_scan(row[:, 4, :], row[:, 3, :], row[:, 5, :], 0.0, ALU.add, ALU.add))
                step(V.tensor_tensor(row[:, 3, :], row[:, 3, :], row[:, 4, :], ALU.subtract))
                step(V.tensor_tensor(row[:, 3, :], row[:, 3, :], row[:, 2, :], ALU.add))
                step(V.memset(row[:, 2, :], 0.0))
                step(V.tensor_tensor(row[:, 2, 0:NT - 1], row[:, 3, 1:NT], row[:, 3, 0:NT - 1], ALU.subtract))
                for c, r in ((0, 4), (1, 2)):
                    step(V.tensor_tensor(row[0:NT, 7, 0:NT], row[0:NT, r, 0:NT], ident[0:NT, 0:NT], ALU.mult))
                    step(V.reduce_sum(col[0:NT, c:c + 1], row[0:NT, 7, 0:NT], axis=AX_X))
                note(V.tensor_scalar(past[0:NT, :], iota[0:NT, 0:J], col[0:NT, 0:1], None, ALU.is_ge))
                step(V.tensor_scalar(colrep[0:NT, :], ones[0:NT, :], col[0:NT, 1:2], None, ALU.mult))
                dve.sem_inc(s_past, 1)
                dve.wait_ge(s_plan_mm, n + 1)
                note(V.tensor_copy(node_t[:, :], ps[:, 2, 0:J]))
                note(V.tensor_scalar(node_p[:, 0:J], ps[:, 2, 0:J], float(P), None, ALU.mult))
                step(V.tensor_tensor(grp_t[:, :], ps[:, 3, 0:J], iota[:, 0:J], ALU.add))
                step(V.tensor_scalar(grp_t[:, :], grp_t[:, :], float(NG - 1), None, ALU.min))
                step(V.tensor_scalar(past[:, :], grp_t[:, :], iota_p[:, 0:1], None, ALU.is_le))
                step(V.reduce_sum(upto[:, :], past[:, :], axis=AX_X))
                dve.sem_inc(s_upto, 1)
                floor_of(grp_m[:, :], grp_t[:, :], S)
                step(V.scalar_tensor_tensor(grp_m[:, :], grp_m[:, :], -float(S), grp_t[:, :], ALU.mult, ALU.add))
                note(V.tensor_scalar(steps_i[0:1, 0:J, 0], node_t[0:1, :], float(width), None, ALU.mult))
                note(V.tensor_scalar(steps_i[0:1, 0:J, 1], grp_t[0:1, :], float(H), None, ALU.mult))
                note(V.tensor_scalar(steps_i[0:1, 0:J, 2], grp_m[0:1, :], float(H * D), None, ALU.mult))
                note(V.tensor_scalar(steps_i[0:1, 0:J, 3], grp_t[0:1, :], 1.0, None, ALU.add))
                dve.wait_ge(s_upto_mm, n + 1)
                note(V.tensor_copy(free_i[0:1, :], ps[0:1, 2, 0:P]))
                dve.wait_ge(s_exp, n + 1)
                for c, (a, z) in enumerate(((0, 512), (512, C))):
                    note(V.tensor_copy(ttyp[:, a:z], ps[:, 4 + c, 0:z - a]))
                    note(V.tensor_copy(tkey[:, a:z], ps[:, 6 + c, 0:z - a]))
                settle()
                rounded(tbuf, ttyp[:, :], -7.5, 1.0 / R)
                note(V.tensor_copy(tidx[:, 0:C], tbuf))
                step(V.scalar_tensor_tensor(ttyp[:, :], tbuf, -float(R), ttyp[:, :], ALU.mult, ALU.add))
                dve.sem_inc(s_plan_rd, 1)

            def one_hot(out_ap, numbers, keys, width):
                return V.tensor_tensor(
                    out_ap, numbers[:, 0:width].rearrange("p (a v) -> p a v", a=1).to_broadcast([P, H, width]),
                    keys.rearrange("p (k a) -> p k a", a=1).to_broadcast([P, H, width]), ALU.is_equal)

            def hots(n, j, h, tiles, load=None):
                V.tensor_scalar(klo[:, h, :], tkey[:, bass.ds(tiles, H)], node_p[:, bass.ds(j, 1)], None,
                                ALU.subtract).then_inc(s_klo[n], 1)
                dve.wait_ge(s_klo[n], j + 1)
                one_hot(onehot[:, h], iota, klo[:, h, :], P).then_inc(s_oh[n], 1)
                loaded = load() if load else None
                if n == 0:
                    one_hot(onetyp[:, h], iota, ttyp[:, bass.ds(tiles, H)], R).then_inc(s_oh[n], 1)
                return loaded

            def walk(n, sums, width, first, last, beside=None, noted=0):
                def sums_at(j):
                    return dve.value_load(steps_v[0:1, bass.ds(j * 4, 1)], min_val=0, max_val=NT * width)

                def tiles_of(j):
                    return dve.value_load(steps_v[0:1, bass.ds(j * 4 + 1, 1)], min_val=0, max_val=C - H)

                if first == 0:
                    dve.sem_inc(s_acc[n], 2)
                    for j in range(2):
                        hots(n, j, j, tiles_of(j))
                before_loop = own.value()
                with dve.Fori(first // U, last // U) as i:
                    if noted:
                        own.base, own.k = (i - first // U) * noted + before_loop, 0
                    tiles = tiles_of(i * U + 2)
                    for u in range(U):
                        j, h = i * U + u, u % 2
                        if beside:
                            beside(i, u)
                        at = hots(n, j + 2, (u + 2) % U, tiles, lambda: sums_at(j))
                        if u < U - 1:
                            tiles = tiles_of(j + 3)
                        dve.wait_ge(s_mm[n], j + 1)
                        dve.wait_ge(s_acc[n], j + 2)
                        dest = sums[:, bass.ds(at, width)]
                        V.tensor_tensor(dest, dest, ps[:, h, 0:width], ALU.add).then_inc(s_acc[n], 1)
                if noted:
                    assert own.k == noted
                    own.base, own.k = before_loop + (last - first) // U * noted, 0

            def degree_hots(d, h):
                dve.wait_ge(s_deg_mm, d + 1)
                for out_ap, keys, width in ((oh_lo[:, h], lo1, P), (oh_hi[:, h], hi1, NT)):
                    one_hot(out_ap, iota_bf, keys[:, bass.ds(d * H, H)], width).then_inc(s_deg_oh, 1)

            def ranks_and_degrees(i, u):
                degree_hots(i * U + u, u % 2)
                if u % 2 == 0:
                    rank_a(1, i * (U // 2) + u // 2)
                else:
                    rank_b()

            def moments(value):
                step(V.bn_stats(st[:, :], y[:, :]))
                dve.sem_inc(s_vgo, 1)
                step(V.bn_aggr(mv[:, :], st[:, :]))
                V.tensor_scalar(ve[:, :], mv[:, 1:2], EPS, None, ALU.add).then_inc(s_ve, 1)
                dve.wait_ge(s_rs, value)

            def bring(t):
                dve.wait_ge(s_rkrel, t + 1)
                V.tensor_copy(red[:, :], sums0[:, bass.ds(t * W0, W0)]).then_inc(s_redr, 1)

            def gru(t, k):
                dve.wait_ge(s_gates, t + 2)
                V.tensor_tensor(gate[:, :], ps[:, 2, :], bias[:, 0:2 * D], ALU.add).then_inc(s_rz, 1)
                note(V.tensor_tensor(tA[:, :], ps[:, 3, 0:D], bias[:, 2 * D:3 * D], ALU.add))
                note(V.tensor_tensor(hn[:, :], ps[:, 3, D:2 * D], bias[:, 3 * D:4 * D], ALU.add))
                settle()
                bring(t + 1)
                dve.wait_ge(s_rzs, t + 1)
                step(V.scalar_tensor_tensor(tB[:, :], gate[:, 0:D], 1.0, hn[:, :], ALU.add, ALU.mult))
                V.scalar_tensor_tensor(tA[:, :], tB[:, :], 0.5, tA[:, :], ALU.mult, ALU.add).then_inc(s_npre, 1)
                dve.wait_ge(s_n, t + 1)
                step(V.tensor_tensor(y[:, :], xt[:, k, :], tB[:, :], ALU.subtract))
                step(V.scalar_tensor_tensor(y[:, :], gate[:, D:2 * D], 1.0, y[:, :], ALU.add, ALU.mult))
                step(V.scalar_tensor_tensor(y[:, :], y[:, :], 0.5, tB[:, :], ALU.mult, ALU.add))
                step(V.tensor_tensor(y[:, :], y[:, :], xt[:, k, :], ALU.add))
                moments(t + 1)
                note(V.tensor_scalar(sums0[:, bass.ds(t * W0, D)], y[:, :], mv[:, 0:1], rs[:, :],
                                     ALU.subtract, ALU.mult))
                dve.wait_ge(s_x1tr, t + 1)
                V.tensor_scalar(x1c[:, :], y[:, :], mv[:, 0:1], rs[:, :], ALU.subtract, ALU.mult).then_inc(s_x1, 1)
            GRU_STEPS = 10

            def put_g(t, stored, k):
                dve.wait_ge(s_h, t + 2)
                note(V.tensor_scalar(sums1[:, bass.ds(t * D, D)], ps[:, 5, 0:D], deg_rs[:, bass.ds(t, 1)], None,
                                     ALU.mult))
                dve.wait_ge(s_gst[k], stored * 16 + 16)
                V.tensor_scalar(gt[:, k, :], ps[:, 5, 0:D], deg_rs[:, bass.ds(t, 1)], None,
                                ALU.mult).then_inc(s_g, 1)

            def finish(i):
                def tile(s, width):
                    return bass.ds(i * (FG * width) + s * width, width)

                for s in range(FG):
                    note(V.scalar_tensor_tensor(sums1[:, tile(s, D)], sums1[:, tile(s, D)], deg_rs[:, tile(s, 1)],
                                                sums0[:, bass.ds(i * (FG * W0) + s * W0, D)], ALU.mult, ALU.add))
                settle()
                dve.sem_inc(s_vgo, 1)
                for s in range(FG):
                    note(V.bn_stats(st_all[:, s, :], sums1[:, tile(s, D)]))
                settle()
                dve.sem_inc(s_vgo, 1)
                for s in range(FG):
                    note(V.bn_aggr(mv_all[:, s, :], st_all[:, s, :]))
                settle()
                V.tensor_scalar(ve_all[:, bass.ds(i * FG, FG)], mv_all[:, :, 1], EPS, None, ALU.add).then_inc(s_var, 1)
                note(V.tensor_scalar(mean_all[:, bass.ds(i * FG, FG)], mv_all[:, :, 0], -1.0, None, ALU.mult))
                settle()
            FINISH_STEPS = 3 * FG + 1

            def shift(i):
                dve.wait_ge(s_root, i + 1)
                V.tensor_tensor(mean_all[:, bass.ds(i * FG, FG)], mean_all[:, bass.ds(i * FG, FG)],
                                rs_all[:, bass.ds(i * FG, FG)], ALU.mult).then_inc(s_shift, 1)

            V.memset(zero_bf[:, :], 0.0).then_inc(s_zero, 1)
            note(V.memset(steps_i[:, :, :], 0))
            step(V.memset(node_p[:, J:J + 2], 0.0))
            dve.sem_inc(s_npre, 1)
            dve.sem_inc(s_g, 1)
            dve.wait_ge(s_const, 6)
            dve.wait_ge(s_edges, 128)
            note(V.memset(signs[:, 0:1], float(C)))
            note(V.tensor_scalar(past_by, iota[:, 0:B], -1.0, -0.5, ALU.mult, ALU.add))
            prepare(1)
            dve.sem_inc(s_hi1, 1)
            note(V.tensor_copy(scan, dst_i))
            step(V.tensor_copy(pos, next_i))
            step(V.tensor_tensor(mask, scan, pos, ALU.is_gt))
            step(V.reduce_sum(flag[:, 0:1], mask, axis=AX_X))
            dve.sem_inc(s_flag_in, 1)
            prepare(0)
            count(0)
            dve.wait_ge(s_flag_mm, 1)
            step(V.tensor_scalar(flag_i[0:1, :], ps[0:1, 1, 0:1], 0.0, None, ALU.is_gt))
            dve.sem_inc(s_flag, 1)
            bucket_ends(0)
            unsorted = dve.value_load(flag_i[0:1, 0:1], min_val=0, max_val=1)
            with dve.If(unsorted > 0):
                order[0] = sort
                step(V.memset(pos, -1.0))
                with dve.Fori(0, B) as b:
                    sort.enter(b, 4)
                    rank_a(0, b)
                    rank_b()
                sort.leave(B)
                step(V.tensor_copy(pos_is[0], pos))
                order[0] = own
            dve.sem_inc(s_pos[0], 1)
            plan(0, W0)
            dve.wait_ge(s_sign, B + 1)
            step(V.tensor_tensor(counts[:, 1, :], signs[:, 0:B], signs[:, 1:B + 1], ALU.subtract))
            step(V.tensor_scalar(counts[:, 1, :], counts[:, 1, :], 0.5, None, ALU.mult))
            dve.sem_inc(s_cnt[1], 1)
            bucket_ends(1)
            dve.wait_ge(s_wtr, 28)
            note(V.memset(sums0[:, :], 0.0))
            note(V.memset(sums1[:, NT * D:B * D], 0.0))
            step(V.memset(pos, -1.0))
            dve.sem_inc(s_deg_mm, 2)
            walk(0, sums0, W0, 0, 2 * RANKS, ranks_and_degrees, 2 * U)
            step(V.tensor_copy(pos_is[1], pos))
            dve.sem_inc(s_pos[1], 1)
            dve.wait_ge(s_deg_mm, NG + 3)
            V.tensor_scalar(deg_rs[:, :], ps[:, 7, 0:NT], 1.0, None, ALU.add).then_inc(s_deg1, 1)
            walk(0, sums0, W0, 2 * RANKS, J)
            dve.wait_ge(s_acc[0], J + 2)
            dve.wait_ge(s_bias, 3)
            bring(0)
            gru(0, 0)
            dve.wait_ge(s_degr, 1)
            with dve.Fori(0, NT // 2) as i:
                own.enter(i, 2 * (GRU_STEPS + 1))
                for k in range(2):
                    gru(i * 2 + (k + 1), 1 - k)
                    put_g(i * 2 + k, i, k)
            own.leave(NT // 2)
            put_g(NT - 1, NT // 2, 0)
            settle()
            plan(1, D)
            walk(1, sums1, D, 0, J)
            dve.wait_ge(s_acc[1], J + 2)
            finish(0)
            with dve.Fori(1, NT // FG) as i:
                own.enter(i - 1, FINISH_STEPS)
                finish(i)
                shift(i - 1)
            own.leave(NT // FG - 1)
            shift(NT // FG - 1)

        @block.scalar
        def _(act):
            A = nc.scalar
            act.sem_inc(s_cnT, 1)
            act.sem_inc(s_redt, 1)
            act.sem_inc(s_x1T, 1)
            act.sem_inc(s_wcp, 4)
            at = 0
            for dest in weight_tiles():
                act.wait_ge(s_wtr, at + 1)
                A.copy(dest, ps[:, 4 + at % 4, 0:P]).then_inc(s_wcp, 1)
                at += 1
            for m, (bank, first, size) in enumerate(((4, 0, 2 * D), (5, 2 * D, D), (6, 3 * D, D))):
                act.wait_ge(s_bias_mm, m + 1)
                A.copy(bias[:, first:first + size], ps[:, bank, 0:size]).then_inc(s_bias, 1)

            act.sem_inc(s_sign, 1)
            act.wait_ge(s_hi1, 1)
            with act.Fori(0, B) as b:
                act.wait_ge(s_sign, b + 1)
                A.activation(sides, hi1, ACT.Sign, bias=past_by[:, bass.ds(b, 1)],
                             accum_out=signs[:, bass.ds(b + 1, 1)]).then_inc(s_sign, 1)

            def front(t):
                act.wait_ge(s_xtr, t + 1)
                act.wait_ge(s_gates, t + 1)
                A.copy(xT[:, :], ps[:, 0, 0:D]).then_inc(s_xT, 1)
                A.copy(cnT[:, :], ps[0:R, 0, D:D + P]).then_inc(s_cnT, 1)
                act.wait_ge(s_rkrel, t + 2)
                A.copy(redT[:, :], ps[:, 1, 0:D]).then_inc(s_redt, 1)
                act.wait_ge(s_rz, t + 1)
                A.activation(gate[:, :], gate[:, :], ACT.Tanh, scale=0.5).then_inc(s_rzs, 1)
                act.wait_ge(s_npre, t + 2)
                A.activation(tB[:, :], tA[:, :], ACT.Tanh).then_inc(s_n, 1)

            def back(t):
                act.wait_ge(s_x1tr, t + 2)
                act.wait_ge(s_h, t + 1)
                A.copy(x1T[:, :], ps[:, 4, 0:D]).then_inc(s_x1T, 1)

            def arrivals(n):
                with act.Fori(0, NG // S) as i:
                    for s in range(S):
                        for k in range(H):
                            act.wait_ge(s_rows[s * H + k], i * 16 + (n * NG // S * 16 + 16))
                        act.sem_inc(s_grp[n], 1)

            arrivals(0)
            front(0)
            with act.Fori(0, NT // 2) as i:
                for k in range(2):
                    front(i * 2 + (k + 1))
                    back(i * 2 + k)
            back(NT - 1)
            arrivals(1)
            with act.Fori(0, NT // FG) as i:
                act.wait_ge(s_shift, i + 1)
                for s in range(FG):
                    part = sums1[:, bass.ds(i * (FG * D) + s * D, D)]
                    A.activation(part, part, ACT.Identity, bias=mean_all[:, bass.ds(i * FG + s, 1)],
                                 scale=rs_all[:, bass.ds(i * FG + s, 1)]).then_inc(s_o, 1)

        @block.tensor
        def _(pe):
            M = nc.tensor
            pe.sem_inc(s_gates, 1)
            pe.sem_inc(s_x1tr, 1)
            pe.sem_inc(s_h, 1)
            pe.sem_inc(s_rkrel, 1)
            pe.wait_ge(s_const, 6)
            pe.wait_ge(s_w, 64)
            blocks = [wnat[:, a, k, c * P:(c + 1) * P] for a in range(2) for k in range(G3 // P) for c in range(2)]
            blocks += [w1nat[:, k, c * P:(c + 1) * P] for k in range(2) for c in range(2)]
            for at, b in enumerate(blocks):
                pe.wait_ge(s_wcp, at + 1)
                M.transpose(ps[:, 4 + at % 4, 0:P], b, ident[:, :]).then_inc(s_wtr, 1)
            pe.wait_ge(s_wcp, len(blocks) + 4)
            pe.wait_ge(s_brow, 32)
            one = ones[0:1, :]
            M.matmul(ps[:, 4, :], one, brow[0:1, 0:2 * D], start=True, stop=False)
            M.matmul(ps[:, 4, :], one, brow[0:1, G3:G3 + 2 * D], start=False, stop=True).then_inc(s_bias_mm, 1)
            M.matmul(ps[:, 5, 0:D], one, brow[0:1, 2 * D:G3], start=True, stop=True).then_inc(s_bias_mm, 1)
            M.matmul(ps[:, 6, 0:D], one, brow[0:1, G3 + 2 * D:2 * G3], start=True, stop=True).then_inc(s_bias_mm, 1)
            pe.wait_ge(s_flag_in, 1)
            M.matmul(ps[:, 1, 0:1], ones[:, :], flag[:, 0:1], start=True, stop=True).then_inc(s_flag_mm, 1)

            def count(n):
                pe.wait_ge(s_cnt[n], 1)
                M.matmul(ps[:, 2, 0:B], ones[:, :], counts[:, n, :], start=True, stop=True)
                M.matmul(ps[:, 3, 0:B], before, counts[:, n, :], start=True, stop=True).then_inc(s_cnt_mm[n], 1)

            def plan(n):
                pe.wait_ge(s_past, n + 1)
                M.matmul(ps[:, 2, 0:J], ones[0:NT, :], past[0:NT, :], start=True, stop=True)
                M.matmul(ps[:, 3, 0:J], colrep[0:NT, :], past[0:NT, :], start=True, stop=True).then_inc(s_plan_mm, 1)
                pe.wait_ge(s_upto, n + 1)
                M.matmul(ps[0:1, 2, 0:P], upto[:, 0:1], ident[:, :], start=True, stop=True).then_inc(s_upto_mm, 1)
                pe.wait_ge(s_chunk, 16 * KC * (n + 1))
                pe.wait_ge(s_bias, 3)
                for w in range(2):
                    for k, r in enumerate(KROWS):
                        bank, a = 4 + 2 * w + k * P // 512, k * P % 512
                        last = M.matmul(ps[:, bank, a:a + r], chunk[0:r, k, :, w], ident[0:r, 0:r],
                                        start=True, stop=True)
                last.then_inc(s_exp, 1)

            def walk(n, first, last, beside=None):
                with pe.Fori(first // U, last // U) as i:
                    for u in range(U):
                        j, h = i * U + u, u % 2
                        at = pe.value_load(steps_v[0:1, bass.ds(j * 4 + 2, 1)], min_val=0, max_val=(S - 1) * H * D)
                        group = pe.value_load(steps_v[0:1, bass.ds(j * 4 + 3, 1)], min_val=1, max_val=NG)
                        pe.wait_ge(s_acc[n], j + 1)
                        pe.wait_ge(s_oh[n], (j + 1) * (2 - n))
                        pe.wait_ge(s_grp[n], group)
                        for k in range(H):
                            prod = M.matmul(ps[:, h, 0:D], onehot[:, u, k, :], rows[:, bass.ds(at + k * D, D)],
                                            start=(k == 0), stop=(k == H - 1))
                        if n == 0:
                            for k in range(H):
                                prod = M.matmul(ps[:, h, D:W0], onehot[:, u, k, :], onetyp[:, u, k, :],
                                                start=(k == 0), stop=(k == H - 1))
                        prod.then_inc(s_mm[n], 1)
                        if beside:
                            beside(i, u)

            def degrees(d, h):
                pe.wait_ge(s_deg_oh, (d + 1) * 2)
                for k in range(H):
                    cnt = M.matmul(ps[:, 7, 0:NT], oh_lo[:, h, k, :], oh_hi[:, h, k, :], start=False, stop=False)
                cnt.then_inc(s_deg_mm, 1)

            def front(t, loaded, k):
                pe.wait_ge(s_x[k], loaded * 16 + 16)
                pe.wait_ge(s_redr, t + 1)
                pe.wait_ge(s_cnT, t + 1)
                for c in range(2):
                    M.transpose(ps[:, 0, c * P:c * P + P], xt[:, k, c * P:c * P + P], ident[:, :])
                M.transpose(ps[0:R, 0, D:D + P], red[:, D:W0], ident[:, :]).then_inc(s_xtr, 1)
                pe.wait_ge(s_cnT, t + 2)
                pe.wait_ge(s_redt, t + 1)
                for c in range(2):
                    M.matmul(ps[:, 1, c * P:c * P + P], red[:, c * P:c * P + P], ident[:, :], start=True, stop=False)
                    last = M.matmul(ps[:, 1, c * P:c * P + P], rel_s[:, c * P:c * P + P], cnT[:, :],
                                    start=False, stop=True)
                last.then_inc(s_rkrel, 1)
                pe.wait_ge(s_npre, t + 1)
                pe.wait_ge(s_redt, t + 2)
                parts = [(m[:, c * P:c * P + P], wT[:, a, c, :]) for a, m in ((1, xT), (0, redT)) for c in range(2)]
                for q, (lhs, w) in enumerate(parts):
                    M.matmul(ps[:, 2, :], lhs, w[:, 0:2 * D], start=(q == 0), stop=(q == 3))
                for a, cols in ((1, slice(D, 2 * D)), (0, slice(0, D))):
                    for c in range(2):
                        lhs, w = parts[(1 - a) * 2 + c]
                        last = M.matmul(ps[:, 3, cols], lhs, w[:, 2 * D:G3], start=(c == 0), stop=(c == 1))
                last.then_inc(s_gates, 1)

            def back(t):
                pe.wait_ge(s_x1, t + 1)
                pe.wait_ge(s_x1T, t + 1)
                for c in range(2):
                    last = M.transpose(ps[:, 4, c * P:c * P + P], x1c[:, c * P:c * P + P], ident[:, :])
                last.then_inc(s_x1tr, 1)
                pe.wait_ge(s_g, t + 1)
                pe.wait_ge(s_x1T, t + 2)
                for c in range(2):
                    last = M.matmul(ps[:, 5, 0:D], x1T[:, c * P:c * P + P], w1T[:, c, :], start=(c == 0), stop=(c == 1))
                last.then_inc(s_h, 1)

            count(0)
            plan(0)
            pe.wait_ge(s_plan_rd, 1)
            count(1)
            pe.wait_ge(s_zero, 1)
            M.matmul(ps[:, 7, 0:NT], zero_bf[:, :], zero_bf[:, 0:NT], start=True, stop=False)
            walk(0, 0, 2 * RANKS, lambda i, u: degrees(i * U + u, u % 2))
            M.matmul(ps[:, 7, 0:NT], zero_bf[:, :], zero_bf[:, 0:NT], start=False, stop=True).then_inc(s_deg_mm, 1)
            walk(0, 2 * RANKS, J)
            front(0, 0, 0)
            with pe.Fori(0, NT // 2) as i:
                for k in range(2):
                    front(i * 2 + (k + 1), i + k, 1 - k)
                    back(i * 2 + k)
            back(NT - 1)
            plan(1)
            pe.wait_ge(s_plan_rd, 2)
            walk(1, 0, J)


_INS = ['x', 'src', 'dst', 'edge_type_16', 'L0_gnn_relvectors', 'L0_gnn_w_ih', 'L0_gnn_w_hh', 'L0_gnn_b_ih',
        'L0_gnn_b_hh', 'L1_gnn_W']


def kernel(**inputs):
    import numpy as _np
    import concourse.bacc as _bacc
    from concourse import mybir as _mybir
    from concourse.bass_utils import run_bass_kernel_spmd as _run

    nc = _bacc.Bacc("TRN2", target_bir_lowering=False, num_devices=1)
    arrays, args = {}, []
    for name in _INS:
        a = _np.ascontiguousarray(inputs[name])
        arrays[f"in_{name}_dram"] = a
        args.append(nc.dram_tensor(f"in_{name}_dram", a.shape, _mybir.dt.from_np(a.dtype), kind="ExternalInput").ap())
    f32 = _mybir.dt.float32
    args.append(nc.dram_tensor("out_0_dram", (N, D), f32, kind="ExternalOutput").ap())
    for name, shape in (("table0", (C * P, 2)), ("table1", (C * P, 2)), ("gdram", (N, D))):
        args.append(nc.dram_tensor(name, shape, f32, kind="Internal").ap())
    build(nc, *args)
    r = _run(nc, [arrays], core_ids=[0])
    return r.results[0]["out_0_dram"]
```
